# Optimizing a Trainium2 kernel written in Bass

```python
import numpy as np
import jax
import jax.numpy as jnp

def _softmax(x, axis=-1):
    return jax.nn.softmax(x, axis=axis)

def _gelu(x):
    return jax.nn.gelu(x, approximate=True)

def _silu(x):
    return jax.nn.silu(x)

def _sigmoid(x):
    return jax.nn.sigmoid(x)

def _layernorm(x, axis=-1, eps=1e-05):
    m = jnp.mean(x, axis=axis, keepdims=True)
    v = jnp.var(x, axis=axis, keepdims=True)
    return (x - m) / jnp.sqrt(v + eps)

def _scatter_add(tgt, idx, src, axis=0):
    return tgt.at[idx].add(src)

def _segment_sum(src, seg, n):
    return jax.ops.segment_sum(src, seg, n)
kernel_name = 'mk_gnn_preln_d4_gnn_r32_b36eef'

def setup_inputs(seed: int=0):
    np.random.seed(seed)
    _w = jnp.asarray

    def _rec_inputs():
        import jax
        import jax.numpy as jnp
        _gk = jax.random.key(seed)
        x = -0.000202 + 1 * jax.random.normal(jax.random.fold_in(_gk, 1), (3125, 64), jnp.float32)
        _s = jax.random.randint(jax.random.fold_in(_gk, 2), (25000,), 0, 3125, jnp.int32)
        _d = jax.random.randint(jax.random.fold_in(_gk, 3), (25000,), 0, 3125, jnp.int32)
        _loop = jnp.arange(3125, dtype=jnp.int32)
        src = jnp.concatenate([_s, _d, _loop])
        dst = jnp.concatenate([_d, _s, _loop])
        _o = jnp.argsort(dst, stable=True)
        src = src[_o]
        dst = dst[_o]
        edge_attr_64 = 9.41057e-06 + 1 * jax.random.normal(jax.random.fold_in(_gk, 12), (53125, 64), jnp.float32)
        edge_weight = jax.random.uniform(jax.random.fold_in(_gk, 13), (53125,), jnp.float32, 0.0, 1)
        node_vec1 = jax.random.uniform(jax.random.fold_in(_gk, 14), (3125, 1), jnp.float32, 0.0, 0.999993)
        node_vec1_n2 = jax.random.uniform(jax.random.fold_in(_gk, 15), (3125, 1), jnp.float32, 0.0, 0.999993)
        return (x, src, dst, edge_attr_64, edge_weight, node_vec1, node_vec1_n2)
    x, src, dst, edge_attr_64, edge_weight, node_vec1, node_vec1_n2 = _rec_inputs()

    def _L0_gnn_setup():
        import jax, jax.numpy as jnp
        import numpy as np
        K = 10
        ALPHA = 0.1
        N_NODES = 3125
        N_EDGES = 31250
        D_FEAT = 64
        key = jax.random.key(seed)
        k1, k2, k3 = jax.random.split(key, 3)
        feat = jax.random.normal(k1, (N_NODES, D_FEAT), dtype=jnp.float32)
        edge_src = jax.random.randint(k2, (N_EDGES,), 0, N_NODES, dtype=jnp.int32)
        edge_dst = jax.random.randint(k3, (N_EDGES,), 0, N_NODES, dtype=jnp.int32)
        return {'feat': feat, 'edge_src': edge_src, 'edge_dst': edge_dst}
    _L0_gnn_all = _L0_gnn_setup()
    _L0_gnn_in = {k: v for k, v in _L0_gnn_all.items() if k in ()}
    del _L0_gnn_all

    def _L1_gnn_setup():
        import jax, jax.numpy as jnp
        import numpy as np
        N_NODES = 50000
        N_EDGES = 25000
        EMB = 64
        HEADS = 4
        key = jax.random.key(seed)
        k1, k2, k3, k4, k5, k6 = jax.random.split(key, 6)
        scale = 1.0 / np.sqrt(EMB)
        return {'embeds': jax.random.normal(k1, (N_NODES, EMB), dtype=jnp.float32), 'rows': jax.random.randint(k2, (N_EDGES,), 0, N_NODES, dtype=jnp.int64), 'cols': jax.random.randint(k3, (N_EDGES,), 0, N_NODES, dtype=jnp.int64), 'qTrans': jax.random.normal(k4, (EMB, EMB), dtype=jnp.float32) * scale, 'kTrans': jax.random.normal(k5, (EMB, EMB), dtype=jnp.float32) * scale, 'vTrans': jax.random.normal(k6, (EMB, EMB), dtype=jnp.float32) * scale}
    _L1_gnn_all = _L1_gnn_setup()
    _L1_gnn_in = {k: v for k, v in _L1_gnn_all.items() if k in ('qTrans', 'kTrans', 'vTrans')}
    del _L1_gnn_all

    def _L2_gnn_setup():
        import jax, jax.numpy as jnp
        import numpy as np
        N_NODES = 50000
        N_EDGES = 25000
        D_IN = 64
        D_OUT = 64
        key = jax.random.key(seed)
        ks = jax.random.split(key, 8)
        feat = jax.random.normal(ks[0], (N_NODES, D_IN), dtype=jnp.float32)
        weight = jax.random.uniform(ks[1], (N_EDGES,), dtype=jnp.float32)
        W_self = jax.random.normal(ks[2], (D_OUT, D_IN), dtype=jnp.float32) * 0.1
        b_self = jax.random.normal(ks[3], (D_OUT,), dtype=jnp.float32) * 0.1
        W_neigh = jax.random.normal(ks[4], (D_OUT, D_IN), dtype=jnp.float32) * 0.1
        b_neigh = jax.random.normal(ks[5], (D_OUT,), dtype=jnp.float32) * 0.1
        src = jax.random.randint(ks[6], (N_EDGES,), 0, N_NODES, dtype=jnp.int64)
        dst = jax.random.randint(ks[7], (N_EDGES,), 0, N_NODES, dtype=jnp.int64)
        return {'feat': feat, 'weight': weight, 'W_self': W_self, 'b_self': b_self, 'W_neigh': W_neigh, 'b_neigh': b_neigh, 'src': src, 'dst': dst}
    _L2_gnn_all = _L2_gnn_setup()
    _L2_gnn_in = {k: v for k, v in _L2_gnn_all.items() if k in ('W_self', 'b_self', 'W_neigh', 'b_neigh')}
    del _L2_gnn_all

    def _L3_gnn_setup():
        import jax, jax.numpy as jnp
        import numpy as np
        N = 3125
        E = 100000
        D = 64
        key = jax.random.key(seed)
        k = jax.random.split(key, 7)
        weight = jax.random.normal(k[0], (N, D), dtype=jnp.float32) * 0.05
        ps_w = jax.random.normal(k[1], (1, D), dtype=jnp.float32) * 0.1
        review_feat = jax.random.normal(k[2], (E, D), dtype=jnp.float32)
        cj = jax.random.uniform(k[3], (N, 1), dtype=jnp.float32)
        ci = jax.random.uniform(k[4], (N, 1), dtype=jnp.float32)
        src = jax.random.randint(k[5], (E,), 0, N, dtype=jnp.int32)
        dst = jax.random.randint(k[6], (E,), 0, N, dtype=jnp.int32)
        return {'weight': weight, 'ps_w': ps_w, 'review_feat': review_feat, 'cj': cj, 'ci': ci, 'src': src, 'dst': dst}
    _L3_gnn_all = _L3_gnn_setup()
    _L3_gnn_in = {k: v for k, v in _L3_gnn_all.items() if k in ('ps_w',)}
    del _L3_gnn_all
    return {'x': x, 'src': src, 'dst': dst, 'edge_attr_64': edge_attr_64, 'edge_weight': edge_weight, 'node_vec1': node_vec1, 'node_vec1_n2': node_vec1_n2, 'L1_gnn_qTrans': _L1_gnn_in['qTrans'], 'L1_gnn_kTrans': _L1_gnn_in['kTrans'], 'L1_gnn_vTrans': _L1_gnn_in['vTrans'], 'L2_gnn_W_self': _L2_gnn_in['W_self'], 'L2_gnn_b_self': _L2_gnn_in['b_self'], 'L2_gnn_W_neigh': _L2_gnn_in['W_neigh'], 'L2_gnn_b_neigh': _L2_gnn_in['b_neigh'], 'L3_gnn_ps_w': _L3_gnn_in['ps_w']}

def reference(x, src, dst, edge_attr_64, edge_weight, node_vec1, node_vec1_n2, L1_gnn_qTrans, L1_gnn_kTrans, L1_gnn_vTrans, L2_gnn_W_self, L2_gnn_b_self, L2_gnn_W_neigh, L2_gnn_b_neigh, L3_gnn_ps_w):
    import jax
    import jax.numpy as jnp

    def _L0_gnn_ref(feat, edge_src, edge_dst):
        import jax, jax.numpy as jnp
        import numpy as np
        K = 10
        ALPHA = 0.1
        N_NODES = 3125
        N_EDGES = 31250
        D_FEAT = 64
        n = feat.shape[0]
        deg = jax.ops.segment_sum(jnp.ones_like(edge_dst, dtype=feat.dtype), edge_dst, num_segments=n)
        norm = jnp.power(jnp.clip(deg, 1.0, None), -0.5)[:, None]
        feat_0 = feat
        h = feat
        for _ in range(K):
            msg = h[edge_src] * norm[edge_src]
            agg = jax.ops.segment_sum(msg, edge_dst, num_segments=n)
            h = (1.0 - ALPHA) * (agg * norm) + ALPHA * feat_0
        return h

    def _L1_gnn_ref(embeds, rows, cols, qTrans, kTrans, vTrans):
        import jax, jax.numpy as jnp
        import numpy as np
        N_NODES = 50000
        N_EDGES = 25000
        EMB = 64
        HEADS = 4
        n_nodes = embeds.shape[0]
        head_dim = EMB // HEADS
        rowEmb = embeds[rows]
        colEmb = embeds[cols]
        q = (rowEmb @ qTrans).reshape(-1, HEADS, head_dim)
        k = (colEmb @ kTrans).reshape(-1, HEADS, head_dim)
        v = (colEmb @ vTrans).reshape(-1, HEADS, head_dim)
        att = jnp.einsum('ehd,ehd->eh', q, k)
        att = jnp.clip(att, -10.0, 10.0)
        expAtt = jnp.exp(att)
        attNorm = jax.ops.segment_sum(expAtt, rows, num_segments=n_nodes)[rows]
        att = expAtt / (attNorm + 1e-08)
        res = (att[:, :, None] * v).reshape(-1, EMB)
        out = jax.ops.segment_sum(res, rows, num_segments=n_nodes)
        return out

    def _L2_gnn_ref(feat, weight, W_self, b_self, W_neigh, b_neigh, src, dst):
        import jax, jax.numpy as jnp
        import numpy as np
        N_NODES = 50000
        N_EDGES = 25000
        D_IN = 64
        D_OUT = 64
        n = feat.shape[0]
        msg = feat[src] * weight[:, None]
        neigh_sum = jax.ops.segment_sum(msg, dst, num_segments=n)
        deg = jax.ops.segment_sum(jnp.ones_like(weight), dst, num_segments=n)
        h_neigh = neigh_sum / jnp.maximum(deg, 1.0)[:, None]
        rst = feat @ W_self.T + b_self + (h_neigh @ W_neigh.T + b_neigh)
        return rst

    def _L3_gnn_ref(weight, ps_w, review_feat, cj, ci, src, dst):
        import jax, jax.numpy as jnp
        import numpy as np
        N = 3125
        E = 100000
        D = 64
        feat = weight * cj
        pa = jax.nn.sigmoid(review_feat @ ps_w.T)
        msg = pa * feat[src]
        h = jax.ops.segment_sum(msg, dst, num_segments=weight.shape[0])
        return h * ci
    h = jnp.maximum(_layernorm(x, axis=-1), 0.0)
    x = x + _L0_gnn_ref(h, src, dst)
    h = jnp.maximum(_layernorm(x, axis=-1), 0.0)
    x = x + _L1_gnn_ref(h, src, dst, L1_gnn_qTrans, L1_gnn_kTrans, L1_gnn_vTrans)
    h = jnp.maximum(_layernorm(x, axis=-1), 0.0)
    x = x + _L2_gnn_ref(h, edge_weight, L2_gnn_W_self, L2_gnn_b_self, L2_gnn_W_neigh, L2_gnn_b_neigh, src, dst)
    h = jnp.maximum(_layernorm(x, axis=-1), 0.0)
    x = x + _L3_gnn_ref(h, L3_gnn_ps_w, edge_attr_64, node_vec1, node_vec1_n2, src, dst)
    return x

_drawn_inputs = setup_inputs


def setup_inputs(seed=0):
    import zlib

    import numpy as np

    out = dict(_drawn_inputs(seed))
    spreads = {}
    factors = {'edge_weight': 2.773}
    for name, (base, spread) in spreads.items():
        noise = np.random.default_rng([zlib.crc32(name.encode()), seed]).standard_normal(out[name].shape)
        drawn = base * np.exp(spread * noise) if base else spread * noise
        out[name] = jnp.asarray(drawn.astype(out[name].dtype))
    for name, factor in factors.items():
        out[name] = (out[name] * factor).astype(out[name].dtype)
    return out
```

```python
import concourse.bass as bass
from concourse import mybir
from contextlib import ExitStack

F32, I32, U32 = mybir.dt.float32, mybir.dt.int32, mybir.dt.uint32
ALU, ACT, AX = mybir.AluOpType, mybir.ActivationFunctionType, mybir.AxisListType

N, E, D = 3125, 53125, 64
P = 125
T = N // P
J = E // P
HEADS, HD = 4, D // 4
M1 = D + HEADS
TB = 7
NBANK = -(-T // TB)
K0, ALPHA, EPS = 10, 0.1, 1e-5
CJ = 25
ROUND = 12582912.0


def graph_net(nc, x, src, dst, edge_attr, edge_weight, cj, ci,
              wq, wk, wv, w_self, b_self, w_neigh, b_neigh, ps_w, out):
    ctx = ExitStack()
    with ctx:
        def sb(name, shape, dt=F32):
            return ctx.enter_context(nc.sbuf_tensor(name, shape, dt))

        def sem(name):
            return ctx.enter_context(nc.semaphore(name))

        g_table = nc.dram_tensor("g_table", [N, D], F32).ap()
        kv_table = nc.dram_tensor("kv_table", [N, 2 * D], F32).ap()

        xs = sb("xs", [P, T, D])
        h = sb("h", [P, T, D])
        sq = sb("sq", [P, T, D])
        base = sb("base", [P, T, D])
        agg = sb("agg", [P, NBANK * TB, M1])
        kvs = sb("kvs", [P, T, 3 * D])
        mean = sb("mean", [P, T])
        var = sb("var", [P, T])
        std = sb("std", [P, T])
        rstd = sb("rstd", [P, T])
        deg = sb("deg", [P, T])
        norm = sb("norm", [P, T])
        rdeg = sb("rdeg", [P, T])
        coef = sb("coef", [P, T])
        cjs = sb("cjs", [P, T])
        cis = sb("cis", [P, T])
        wqkv = sb("wqkv", [D, 3 * D])
        w2raw = sb("w2raw", [D, 2 * D])
        w2 = sb("w2", [D, 2 * D])
        bias2 = sb("bias2", [1, 2 * D])
        hT = sb("hT", [D, T, P])
        nT = sb("nT", [D, T, P])
        psw = sb("psw", [P, D])
        ident = sb("ident", [128, 128])
        ones = sb("ones", [128, 128])
        zeros = sb("zeros", [P, 512])

        src_i = sb("src_i", [P, J], I32)
        dst_i = sb("dst_i", [P, J], I32)
        dst_f = sb("dst_f", [P, J])
        w_e = sb("w_e", [P, J])
        z_e = sb("z_e", [P, J])
        pa_e = sb("pa_e", [P, J])
        ea = sb("ea", [P, 2, CJ, D])

        node_i = sb("node_i", [P, N], I32)
        node_f = sb("node_f", [P, N])
        hit = sb("hit", [P, N])
        idx_s = sb("idx_s", [P, 1], I32)
        idx_d = sb("idx_d", [P, 1], I32)
        rows = sb("rows", [P, 2 * D])
        rows_q = sb("rows_q", [P, D])
        qk = sb("qk", [P, D])
        att = sb("att", [P, HEADS])
        att2 = sb("att2", [P, HEADS])
        msg = sb("msg", [P, M1])

        acc = ctx.enter_context(nc.psum_tensor("acc", [128, NBANK, 512], F32))
        ps = ctx.enter_context(nc.psum_tensor("ps", [128, 2, 512], F32))

        names = ("x_in", "idx_in", "edge_in", "par_in", "ea_in0", "ea_in1", "pool_step", "vec_step",
                 "var_ready", "std_ready", "z_ready", "pa_ready", "ea_used",
                 "table_ready", "table_in", "idx_ready", "gathered", "msg_ready", "hit_ready",
                 "scattered", "acc_clear", "acc_taken", "logit_ready", "expd",
                 "pt_ready", "pt_taken", "w2_ready", "out_ready", "out_in", "nT_ready", "h_ready", "gather_turn") + tuple(f"gathered{i}" for i in range(1, K0 + 4))
        S = {n: sem(n) for n in names}
        block = ctx.enter_context(nc.Block())

        PASSES = ["deg"] + ["l0"] * K0 + ["l1", "l2", "l3"]
        WIDTH = {"deg": 1, "l0": D, "l1": M1, "l2": D + 1, "l3": D}

        @block.sync
        def _(sp):
            sp.dma_start(src_i[:, :], src.rearrange("(p j) -> p j", p=P)).then_inc(S["idx_in"], 16)
            sp.dma_start(dst_i[:, :], dst.rearrange("(p j) -> p j", p=P)).then_inc(S["idx_in"], 16)
            sp.dma_start(xs[:, :, :], x.rearrange("(t p) f -> p t f", p=P)).then_inc(S["x_in"], 16)
            sp.dma_start(w_e[:, :], edge_weight.rearrange("(p j) -> p j", p=P)).then_inc(S["edge_in"], 16)
            with nc.allow_non_contiguous_dma("node vectors of one column"):
                sp.dma_start(cjs[:, :], cj.rearrange("(t p) o -> p (t o)", p=P)).then_inc(S["par_in"], 16)
                sp.dma_start(cis[:, :], ci.rearrange("(t p) o -> p (t o)", p=P)).then_inc(S["par_in"], 16)
            sp.dma_start(wqkv[:, 0:D], wq).then_inc(S["par_in"], 16)
            sp.dma_start(wqkv[:, D:2 * D], wk).then_inc(S["par_in"], 16)
            sp.dma_start(wqkv[:, 2 * D:], wv).then_inc(S["par_in"], 16)
            sp.dma_start(w2raw[:, 0:D], w_self).then_inc(S["par_in"], 16)
            sp.dma_start(w2raw[:, D:], w_neigh).then_inc(S["par_in"], 16)
            sp.dma_start(bias2[:, 0:D], b_self.rearrange("(o f) -> o f", o=1)).then_inc(S["par_in"], 16)
            sp.dma_start(bias2[:, D:], b_neigh.rearrange("(o f) -> o f", o=1)).then_inc(S["par_in"], 16)
            sp.dma_start(psw[:, :], ps_w.partition_broadcast(P) if len(ps_w.shape) == 1
                         else ps_w.rearrange("o f -> (o f)").partition_broadcast(P)).then_inc(S["par_in"], 16)
            ea_v = edge_attr.rearrange("(p j) f -> p j f", p=P)
            for c in range(J // CJ):
                if c >= 2:
                    sp.wait_ge(S["ea_used"], c - 1)
                sp.dma_start(ea[:, c % 2], ea_v[:, c * CJ:(c + 1) * CJ, :]).then_inc(S[f"ea_in{c % 2}"], 16)
            n = 0
            for i, p in enumerate(PASSES):
                if p == "deg":
                    continue
                n += 1
                sp.wait_ge(S["table_ready"], n)
                if p == "l1":
                    sp.dma_start(kv_table.rearrange("(t p) f -> p t f", p=P), kvs[:, :, D:]).then_inc(S["table_in"], 16)
                    sp.dma_start(g_table.rearrange("(t p) f -> p t f", p=P), kvs[:, :, 0:D]).then_inc(S["table_in"], 16)
                else:
                    sp.dma_start(g_table.rearrange("(t p) f -> p t f", p=P), h[:, :, :]).then_inc(S["table_in"], 16)
            sp.wait_ge(S["out_ready"], 1)
            sp.dma_start(out.rearrange("(t p) f -> p t f", p=P), xs[:, :, :]).then_inc(S["out_in"], 16)
            sp.wait_ge(S["out_in"], 16)

        @block.gpsimd
        def _(pool):
            pool.iota(node_i[:, :], pattern=[[1, N]], base=0, channel_multiplier=0).then_inc(S["pool_step"], 1)
            pool.memset(ones[:, :], 1.0).then_inc(S["pool_step"], 1)
            pool.memset(zeros[:, :], 0.0).then_inc(S["pool_step"], 1)
            pool.memset(ident[:, :], 0.0).then_inc(S["pool_step"], 1)
            pool.wait_ge(S["pool_step"], 4)
            pool.affine_select(out=ident[:, :], in_=ident[:, :], compare_op=ALU.not_equal, fill=1.0,
                               base=0, pattern=[[-1, 128]], channel_multiplier=1).then_inc(S["pool_step"], 1)
            step, tab, got = 0, 0, 0
            for n, p in enumerate(PASSES):
                if p != "deg":
                    tab += 32 if p == "l1" else 16
                    pool.wait_ge(S["table_in"], tab)
                    k = 32 if p == "l1" else 16
                    with pool.Fori(0, J) as j:
                        pool.wait_ge(S["idx_ready"], step + 1 + j)
                        pool.sem_inc(S["gather_turn"], 1)
                        if p == "l1":
                            pool.indirect_dma_start(rows[:, :], None, kv_table, bass.IndirectOffsetOnAxis(idx_s[:, :], 0)).then_inc(S[f"gathered{n}"], 16)
                            pool.indirect_dma_start(rows_q[:, :], None, g_table, bass.IndirectOffsetOnAxis(idx_d[:, :], 0)).then_inc(S[f"gathered{n}"], 16)
                        else:
                            pool.indirect_dma_start(rows[:, 0:D], None, g_table, bass.IndirectOffsetOnAxis(idx_s[:, :], 0)).then_inc(S[f"gathered{n}"], 16)
                step += J

        @block.scalar
        def _(act):
            def std_of_var(n):
                act.wait_ge(S["var_ready"], n)
                act.activation(std[:, :], var[:, :], ACT.Sqrt).then_inc(S["std_ready"], 1)
            act.wait_ge(S["z_ready"], 1)
            act.activation(pa_e[:, :], z_e[:, :], ACT.Sigmoid).then_inc(S["pa_ready"], 1)
            std_of_var(1)
            std_of_var(2)
            std_of_var(3)
            with act.Fori(0, J) as j:
                act.wait_ge(S["logit_ready"], j + 1)
                act.activation(msg[:, D:M1], att2[:, :], ACT.Exp).then_inc(S["expd"], 1)
            std_of_var(4)
            std_of_var(5)

        @block.vector
        def _(vec):
            steps = [0]

            def step(ins):
                steps[0] += 1
                ins.then_inc(S["vec_step"], 1)
                vec.wait_ge(S["vec_step"], steps[0])

            def per_node(v):
                return v[:, :].unsqueeze(2).to_broadcast([P, T, D])

            n_norms = [0]

            def std_from_act(v):
                n_norms[0] += 1
                vec.wait_ge(S["std_ready"], n_norms[0])

            def layer_norm():
                step(vec.tensor_reduce(mean[:, :], xs[:, :, :], AX.X, ALU.add))
                step(vec.tensor_scalar(mean[:, :], mean[:, :], 1.0 / D, None, ALU.mult))
                step(vec.tensor_tensor(h[:, :, :], xs[:, :, :], per_node(mean), ALU.subtract))
                step(vec.tensor_tensor(sq[:, :, :], h[:, :, :], h[:, :, :], ALU.mult))
                step(vec.tensor_reduce(var[:, :], sq[:, :, :], AX.X, ALU.add))
                vec.tensor_scalar(var[:, :], var[:, :], 1.0 / D, EPS, ALU.mult, ALU.add).then_inc(S["var_ready"], 1)
                std_from_act(var)
                step(vec.reciprocal(rstd[:, :], std[:, :]))
                step(vec.tensor_tensor(h[:, :, :], h[:, :, :], per_node(rstd), ALU.mult))
                step(vec.tensor_scalar(h[:, :, :], h[:, :, :], 0.0, None, ALU.max))

            done = [0]
            n_deg = [0]

            def aggregate(p):
                b = done[0]
                k = 32 if p == "l1" else 16
                s0, K = steps[0], {"deg": 0, "l0": 0, "l1": 5, "l2": 0, "l3": 0}[p]
                with vec.Fori(0, J) as j:
                    vec.wait_ge(S["scattered"], b + j)
                    vec.tensor_copy(idx_d[:, :], dst_i[:, bass.ds(j, 1)])
                    vec.tensor_copy(idx_s[:, :], src_i[:, bass.ds(j, 1)]).then_inc(S["idx_ready"], 1)
                    vec.tensor_scalar(hit[:, :], node_f[:, :], dst_f[:, bass.ds(j, 1)], None, ALU.is_equal).then_inc(S["hit_ready"], 1)
                    if p == "deg":
                        vec.memset(msg[:, 0:1], 1.0).then_inc(S["msg_ready"], 1)
                    else:
                        vec.wait_ge(S[f"gathered{taken[0]}"], k + j * k)
                    if p == "l0":
                        vec.tensor_copy(msg[:, 0:D], rows[:, 0:D]).then_inc(S["msg_ready"], 1)
                    if p == "l2":
                        vec.memset(msg[:, D:D + 1], 1.0)
                        vec.tensor_scalar(msg[:, 0:D], rows[:, 0:D], w_e[:, bass.ds(j, 1)], None, ALU.mult).then_inc(S["msg_ready"], 1)
                    if p == "l3":
                        vec.tensor_scalar(msg[:, 0:D], rows[:, 0:D], pa_e[:, bass.ds(j, 1)], None, ALU.mult).then_inc(S["msg_ready"], 1)
                    if p == "l1":
                        c = s0 + j * 2
                        vec.tensor_tensor(qk[:, :], rows[:, 0:D], rows_q[:, :], ALU.mult).then_inc(S["vec_step"], 1)
                        vec.wait_ge(S["vec_step"], c + 1)
                        vec.tensor_reduce(att[:, :], qk[:, :].rearrange("p (a d) -> p a d", a=HEADS), AX.X, ALU.add).then_inc(S["vec_step"], 1)
                        vec.wait_ge(S["vec_step"], c + 2)
                        vec.tensor_scalar(att2[:, :], att[:, :], -10.0, 10.0, ALU.max, ALU.min).then_inc(S["logit_ready"], 1)
                        vec.wait_ge(S["expd"], j + 1)
                        vec.tensor_tensor(msg[:, 0:D].rearrange("p (a d) -> p a d", a=HEADS),
                                          rows[:, D:].rearrange("p (a d) -> p a d", a=HEADS),
                                          msg[:, D:M1].unsqueeze(2).to_broadcast([P, HEADS, HD]), ALU.mult).then_inc(S["msg_ready"], 1)
                if p == "l1":
                    steps[0] += 2 * J
                done[0] += J
                vec.wait_ge(S["scattered"], done[0])
                for q in range(NBANK):
                    last = vec.tensor_copy(agg[:, q * TB:(q + 1) * TB, :],
                                    acc[0:P, q, 0:TB * M1].rearrange("p (t f) -> p t f", t=TB))
                    if q == NBANK - 1:
                        last.then_inc(S["acc_taken"], 1)
                taken[0] += 1
                vec.wait_ge(S["acc_taken"], taken[0])

            taken, tables = [0], [0]
            pts = [0]

            def transpose_in(dest_of, n):
                for i in range(n):
                    pts[0] += 1
                    vec.wait_ge(S["pt_ready"], pts[0])
                    dst_ap, src_ap = dest_of(i, (pts[0] - 1) % 2)
                    vec.tensor_copy(dst_ap, src_ap).then_inc(S["pt_taken"], 1)
                vec.wait_ge(S["pt_taken"], pts[0])

            vec.wait_ge(S["idx_in"], 32)
            step(vec.tensor_copy(dst_f[:, :], dst_i[:, :]))
            vec.wait_ge(S["pool_step"], 1)
            step(vec.tensor_copy(node_f[:, :], node_i[:, :]))
            vec.wait_ge(S["par_in"], 160)
            for c in range(J // CJ):
                vec.wait_ge(S[f"ea_in{c % 2}"], 16 * (c // 2 + 1))
                step(vec.tensor_tensor(ea[:, c % 2], ea[:, c % 2], psw[:, :].unsqueeze(1).to_broadcast([P, CJ, D]), ALU.mult))
                vec.tensor_reduce(z_e[:, c * CJ:(c + 1) * CJ], ea[:, c % 2], AX.X, ALU.add).then_inc(S["ea_used"], 1)
            vec.wait_ge(S["ea_used"], J // CJ)
            vec.sem_inc(S["z_ready"], 1)
            vec.wait_ge(S["pa_ready"], 1)
            vec.wait_ge(S["x_in"], 16)
            vec.wait_ge(S["edge_in"], 16)

            layer_norm()
            aggregate("deg")
            step(vec.tensor_scalar(deg[:, :], agg[:, 0:T, 0], 1.0, None, ALU.max))
            step(vec.reciprocal(rdeg[:, :], deg[:, :]))
            vec.tensor_copy(var[:, :], deg[:, :]).then_inc(S["var_ready"], 1)
            std_from_act(deg)
            step(vec.reciprocal(norm[:, :], std[:, :]))
            step(vec.tensor_scalar(coef[:, :], norm[:, :], 1 - ALPHA, None, ALU.mult))
            step(vec.tensor_scalar(base[:, :, :], h[:, :, :], ALPHA, None, ALU.mult))
            for it in range(K0):
                vec.tensor_tensor(h[:, :, :], h[:, :, :], per_node(norm), ALU.mult).then_inc(S["table_ready"], 1)
                tables[0] += 1
                aggregate("l0")
                step(vec.tensor_tensor(h[:, :, :], agg[:, 0:T, 0:D], per_node(coef), ALU.mult))
                step(vec.tensor_tensor(h[:, :, :], h[:, :, :], base[:, :, :], ALU.add))
            step(vec.tensor_tensor(xs[:, :, :], xs[:, :, :], h[:, :, :], ALU.add))

            layer_norm()
            vec.sem_inc(S["h_ready"], 1)
            transpose_in(lambda i, s: (hT[:, i, :], ps[0:D, s, 0:P]), T)
            transpose_in(lambda i, s: (kvs[:, i, :], ps[0:P, s, 0:3 * D]), T)
            vec.sem_inc(S["table_ready"], 1)
            aggregate("l1")
            step(vec.tensor_scalar(agg[:, 0:T, D:M1], agg[:, 0:T, D:M1], 1e-8, None, ALU.add))
            step(vec.reciprocal(agg[:, 0:T, D:M1], agg[:, 0:T, D:M1]))
            for a in range(HEADS):
                step(vec.tensor_tensor(h[:, :, a * HD:(a + 1) * HD], agg[:, 0:T, a * HD:(a + 1) * HD],
                                       agg[:, 0:T, D + a:D + a + 1].to_broadcast([P, T, HD]), ALU.mult))
            step(vec.tensor_tensor(xs[:, :, :], xs[:, :, :], h[:, :, :], ALU.add))

            layer_norm()
            vec.sem_inc(S["table_ready"], 1)
            vec.sem_inc(S["h_ready"], 1)
            transpose_in(lambda i, s: (hT[:, i, :], ps[0:D, s, 0:P]), T)
            aggregate("l2")
            step(vec.tensor_tensor(h[:, :, :], agg[:, 0:T, 0:D], per_node(rdeg), ALU.mult))
            vec.sem_inc(S["h_ready"], 1)
            transpose_in(lambda i, s: (nT[:, i, :], ps[0:D, s, 0:P]), T)
            transpose_in(lambda i, s: (w2[:, i * D:(i + 1) * D], ps[0:D, s, 0:D]), 2)
            vec.sem_inc(S["w2_ready"], 1)
            transpose_in(lambda i, s: (h[:, i, :], ps[0:P, s, 0:D]), T)
            step(vec.tensor_tensor(xs[:, :, :], xs[:, :, :], h[:, :, :], ALU.add))

            layer_norm()
            vec.tensor_tensor(h[:, :, :], h[:, :, :], per_node(cjs), ALU.mult).then_inc(S["table_ready"], 1)
            aggregate("l3")
            step(vec.tensor_tensor(h[:, :, :], agg[:, 0:T, 0:D], per_node(cis), ALU.mult))
            vec.tensor_tensor(xs[:, :, :], xs[:, :, :], h[:, :, :], ALU.add).then_inc(S["out_ready"], 1)

        @block.tensor
        def _(pe):
            done, passes, pts = [0], [0], [0]

            def aggregate(p):
                w = WIDTH[p]
                b = done[0]
                if passes[0]:
                    pe.wait_ge(S["acc_taken"], passes[0])
                for q in range(NBANK):
                    pe.matmul(acc[0:P, q, :], zeros[:, 0:P], zeros[:, :], start=True, stop=True)
                with pe.Fori(0, J) as j:
                    pe.wait_ge(S["msg_ready"], b + 1 + j)
                    pe.wait_ge(S["hit_ready"], b + 1 + j)
                    for t in range(T):
                        last = pe.matmul(acc[0:P, t // TB, (t % TB) * M1:(t % TB) * M1 + w],
                                         hit[:, t * P:(t + 1) * P], msg[:, 0:w], start=False, stop=True,
                                         skip_group_check=True)
                    last.then_inc(S["scattered"], 1)
                done[0] += J
                passes[0] += 1

            def slot():
                s = pts[0] % 2
                if pts[0] >= 2:
                    pe.wait_ge(S["pt_taken"], pts[0] - 1)
                pts[0] += 1
                return s

            def transposes(src_of, n, rows):
                for i in range(n):
                    s = slot()
                    a = src_of(i)
                    pe.transpose(ps[0:D, s, 0:rows], a, ident[0:rows, 0:rows]).then_inc(S["pt_ready"], 1)

            pe.wait_ge(S["pool_step"], 5)
            aggregate("deg")
            for _ in range(K0):
                aggregate("l0")
            pe.wait_ge(S["h_ready"], 1)
            transposes(lambda i: h[:, i, :], T, P)
            pe.wait_ge(S["pt_taken"], pts[0])
            for i in range(T):
                s = slot()
                pe.matmul(ps[0:P, s, 0:3 * D], hT[:, i, :], wqkv[:, :], start=True, stop=True).then_inc(S["pt_ready"], 1)
            aggregate("l1")
            pe.wait_ge(S["h_ready"], 2)
            transposes(lambda i: h[:, i, :], T, P)
            aggregate("l2")
            pe.wait_ge(S["h_ready"], 3)
            transposes(lambda i: h[:, i, :], T, P)
            transposes(lambda i: w2raw[:, i * D:(i + 1) * D], 2, D)
            pe.wait_ge(S["w2_ready"], 1)
            for i in range(T):
                s = slot()
                pe.matmul(ps[0:P, s, 0:D], hT[:, i, :], w2[:, 0:D], start=True, stop=False)
                pe.matmul(ps[0:P, s, 0:D], nT[:, i, :], w2[:, D:], start=False, stop=False)
                pe.matmul(ps[0:P, s, 0:D], ones[0:1, 0:P], bias2[:, 0:D], start=False, stop=False)
                pe.matmul(ps[0:P, s, 0:D], ones[0:1, 0:P], bias2[:, D:], start=False, stop=True).then_inc(S["pt_ready"], 1)
            aggregate("l3")


_INS = ['x', 'src', 'dst', 'edge_attr_64', 'edge_weight', 'node_vec1', 'node_vec1_n2', 'L1_gnn_qTrans',
        'L1_gnn_kTrans', 'L1_gnn_vTrans', 'L2_gnn_W_self', 'L2_gnn_b_self', 'L2_gnn_W_neigh',
        'L2_gnn_b_neigh', 'L3_gnn_ps_w']


def kernel(**inputs):
    import numpy as _np
    import concourse.bacc as _bacc
    from concourse import mybir as _mybir
    from concourse.bass_utils import run_bass_kernel_spmd as _run

    nc = _bacc.Bacc("TRN2", target_bir_lowering=False, num_devices=1)
    arrays, args = {}, []
    for name in _INS:
        a = _np.ascontiguousarray(inputs[name])
        arrays[f"in_{name}_dram"] = a
        args.append(nc.dram_tensor(f"in_{name}_dram", a.shape, _mybir.dt.from_np(a.dtype), kind="ExternalInput").ap())
    args.append(nc.dram_tensor("out_dram", (N, D), F32, kind="ExternalOutput").ap())
    graph_net(nc, *args)
    r = _run(nc, [arrays], core_ids=[0])
    return r.results[0]["out_dram"]
```

```python
import concourse.bass as bass
from concourse import mybir
from contextlib import ExitStack

F32, F16, BF16, I32 = mybir.dt.float32, mybir.dt.float16, mybir.dt.bfloat16, mybir.dt.int32
SIZE = {F32: 4, I32: 4, F16: 2, BF16: 2}
ALU, ACT, AX = mybir.AluOpType, mybir.ActivationFunctionType, mybir.AxisListType

N, E, D = 3125, 53125, 64
P = 125
T = N // P
J = E // P
HEADS, HD = 4, D // 4
M1 = D + HEADS
TB = 7
NBANK = -(-T // TB)
K0, ALPHA, EPS = 10, 0.1, 1e-5
CJ = 25
ROUND = 12582912.0

L = 128
C = T + 1
Q = T * C
QH = Q // 2
QT = -(-Q // L)
GSCALE = 4096.0
CH = 4
NCH = -(-T // CH)
PU, PR = 25, 5
AG = [4] * 6 + [2]
SU = 5


def graph_net(nc, x, src, dst, edge_attr, edge_weight, cj, ci,
              wq, wk, wv, w_self, b_self, w_neigh, b_neigh, ps_w, out):
    ctx = ExitStack()
    with ctx:
        def sb(name, shape, dt=F32):
            return ctx.enter_context(nc.sbuf_tensor(name, shape, dt))

        def sem(name):
            return ctx.enter_context(nc.semaphore(name))

        g_table = nc.dram_tensor("g_table", [N, D], F32).ap()
        kv_table = nc.dram_tensor("kv_table", [N, 2 * D], F32).ap()
        slot_rows = nc.dram_tensor("slot_rows", [3, Q * L], BF16).ap()
        w_table = nc.dram_tensor("w_table", [L * Q, 2], F32).ap()

        xs = sb("xs", [P, T, D])
        h = sb("h", [P, T, D])
        base = sb("base", [P, T, D])
        hl_room = sb("hl_room", [L, C * L])
        part_room = sb("part_room", [L, 3 * QT * L // 2])
        part = part_room[:, 0:2 * CH * P].rearrange("p (a n) -> p a n", a=2)
        sl = sb("sl", [L, Q])
        dl = sb("dl", [L, Q])
        slot_i = sb("slot_i", [P, J], I32)
        wpa = sb("wpa", [P, J, 2])
        mean = sb("mean", [P, T])
        var = sb("var", [P, T])
        std = sb("std", [P, T])
        rstd = sb("rstd", [P, T])
        deg = sb("deg", [P, T])
        norm = sb("norm", [P, T])
        rdeg = sb("rdeg", [P, T])
        coef = sb("coef", [P, T])
        cjs = sb("cjs", [P, T])
        cis = sb("cis", [P, T])
        wqkv = sb("wqkv", [D, 3 * D])
        w2raw = sb("w2raw", [D, 2 * D])
        w2 = sb("w2", [D, 2 * D])
        bias2 = sb("bias2", [1, 2 * D])
        psw = sb("psw", [P, D])
        ident = sb("ident", [L, L])
        ones = sb("ones", [L, L])
        pair = sb("pair", [L, D])
        ones_b = sb("ones_b", [L, 1], BF16)
        lane_i = sb("lane_i", [L, 1], I32)
        lane = sb("lane", [L, 1])
        iota_h = sb("iota_h", [L, Q], F16)
        iota_f = sb("iota_f", [L, P])
        flag = sb("flag", [1, 1], I32)
        cols = sb("cols", [L, 2, 2, C])
        late = sb("late", [L, 2, 2, P], BF16)
        s_idx = sb("s_idx", [P, SU, 1], I32)
        s_val = sb("s_val", [P, SU, 2])

        arena = sb("arena", [L, -(-T * N // 2)])

        class Carver:
            def __init__(self, at=0):
                self.at = at

            def __call__(self, shape, dt=F32):
                n = 1
                for d in shape[1:]:
                    n *= d
                words = -(-n * SIZE[dt] // 4)
                v = arena[0:shape[0], self.at:self.at + words]
                self.at += words
                assert self.at <= -(-T * N // 2)
                if dt != F32:
                    v = v.bitcast(dt)
                v = v[:, 0:n]
                if len(shape) == 3:
                    v = v.rearrange("p (a b) -> p a b", a=shape[1])
                if len(shape) == 4:
                    v = v.rearrange("p (a b c) -> p a b c", a=shape[1], b=shape[2])
                return v

        adj = arena[0:P, :].bitcast(F16)[:, 0:T * N].rearrange("p (s d) -> p s d", s=T)

        hl = hl_room[:, 0:2 * T * D].bitcast(F16).rearrange("p (a t f) -> p a t f", a=2, t=T)
        rowbc = hl_room[0:P, :].bitcast(BF16).rearrange("p (e n) -> p e n", e=2)
        rowT = part_room[:, :].bitcast(BF16).rearrange("p (e c r) -> p e c r", e=3, c=QT)
        adj_oh = hl_room[:, :].bitcast(BF16)[:, 0:2 * 24 * P].rearrange("p (e c r) -> p e c r", e=2, c=24)

        cv = Carver()
        src_i, dst_i = cv([P, J], I32), cv([P, J], I32)
        src_f, dst_f = cv([P, J]), cv([P, J])
        st, dt_ = cv([P, J]), cv([P, J])
        s_l, d_l = cv([P, J]), cv([P, J])
        same, last_run = cv([P, J], F16), cv([P, J], F16)
        hits = cv([P, T, J], F16)
        runs = cv([P, T, J], F16)
        picked = cv([P, T, J], F16)
        rank, over, tmp_j = cv([P, J]), cv([P, J]), cv([P, J])
        place = cv([P, J, 3])
        place_u = cv([P, PU, 3])
        iota_i = cv([L, Q], I32)
        edge_w = cv([P, J])
        blank = cv([L, 2 * Q])
        to_lane = cv([P, PR, L], BF16)
        to_col = cv([P, PR, Q], BF16)
        bits = cv([L, Q])
        bits_a, bits_b = cv([L, Q], I32), cv([L, Q], I32)
        sl_s, dl_s = cv([L, T, C]), cv([L, T, C])
        carry, run_end = cv([P, T]), cv([P, T])
        first_d, first_r, earlier, link_m = cv([P, P]), cv([P, P]), cv([P, P]), cv([P, P])
        bad = cv([P, 4])
        zero_c = cv([P, 512])

        cv = Carver()
        agg = cv([P, NBANK * TB, M1])
        node_end = cv.at
        kvs = cv([P, T, 3 * D])
        hT, nT = cv([D, T, P]), cv([D, T, P])

        g_src, g_dst = cv([P, J], I32), cv([P, J], I32)
        g_srcf = cv([P, J])
        g_dstf, g_w, g_pa, g_z = cv([P, J]), cv([P, J]), cv([P, J]), cv([P, J])
        ea = cv([P, 2, CJ * D])
        node_i, node_f = cv([P, N], I32), cv([P, N])
        hit = cv([P, N])
        idx_s, idx_d = cv([P, 1], I32), cv([P, 1], I32)
        rows, rows_q = cv([P, 2 * D]), cv([P, D])
        qk, att, att2, msg = cv([P, D]), cv([P, HEADS]), cv([P, HEADS]), cv([P, M1])
        zeros = cv([P, 512])

        parts = Carver(arena.shape[1] - T * 3 * 3 * D // 2 - 8)([P, T, 3, 3 * D], BF16)
        cv = Carver(node_end)
        kvs_, resid = cv([P, T * 3 * D]), cv([P, T * 3 * D])
        cv = Carver(node_end)
        G1 = cv([L, 2, C, 3 * D])
        G2 = G1.rearrange("p a c f -> p (a c f)")[:, 0:2 * C * D].rearrange("p (a c f) -> p a c f", a=2, c=C)
        prod = cv([L, C, D])
        logit = cv([L, C, HEADS])
        msg1 = cv([L, 2, C, M1])
        wsl = prod.rearrange("p c f -> p (c f)")[:, 0:2 * Q].rearrange("p (q c) -> p q c", c=2)
        ohT = cv([P, 2, 2, C * L], BF16)
        ohd = cv([L, 2, C, P])
        assert cv.at <= arena.shape[1] - T * 3 * 3 * D // 2 - 8

        ps = ctx.enter_context(nc.psum_tensor("ps", [L, 8, 512], F32))
        acc = ps[:, 2:2 + NBANK, :]

        class Sems(dict):
            def __missing__(self, name):
                self[name] = sem(name)
                return self[name]
        S = Sems()
        block = ctx.enter_context(nc.Block())
        PASSES = ["deg"] + ["l0"] * K0 + ["l1", "l2", "l3"]
        WIDTH = {"deg": 1, "l0": D, "l1": M1, "l2": D, "l3": D}
        GROUPS = {"l1": [2] * (C // 2), "l2": [7, 7, 6, 6], "l3": [7, 7, 6, 6]}
        LAG = {"l1": 2, "l2": 1, "l3": 1}
        RING = 6

        def path(eng):
            eng.wait_ge(S["flag_ready"], 1)
            return eng.value_load(flag[0:1, 0:1], min_val=0, max_val=1)

        def tile_steps(eng, lag, body):
            start = lag
            for d in range(lag):
                body(d, d % 2, d // 2, True, False)
            if (T - start) % 2:
                body(start, start % 2, start // 2, True, True)
                start += 1
            with eng.Fori(0, (T - start) // 2) as i:
                for u in range(2):
                    body(i * 2 + (start + u), (start + u) % 2, i + (start + u) // 2, True, True)
            for d in range(T, T + lag):
                body(d, d % 2, d // 2, False, True)

        @block.sync
        def _(sp):
            sp.dma_start(src_i, src.rearrange("(p j) -> p j", p=P)).then_inc(S["idx_in"], 16)
            sp.dma_start(dst_i, dst.rearrange("(p j) -> p j", p=P)).then_inc(S["idx_in"], 16)
            sp.dma_start(xs[:, :, :], x.rearrange("(t p) f -> p t f", p=P)).then_inc(S["x_in"], 16)
            sp.dma_start(edge_w, edge_weight.rearrange("(p j) -> p j", p=P)).then_inc(S["edge_in"], 16)
            with nc.allow_non_contiguous_dma("node vectors of one column"):
                sp.dma_start(cjs[:, :], cj.rearrange("(t p) o -> p (t o)", p=P)).then_inc(S["par_in"], 16)
                sp.dma_start(cis[:, :], ci.rearrange("(t p) o -> p (t o)", p=P)).then_inc(S["par_in"], 16)
            sp.dma_start(wqkv[:, 0:D], wq).then_inc(S["par_in"], 16)
            sp.dma_start(wqkv[:, D:2 * D], wk).then_inc(S["par_in"], 16)
            sp.dma_start(wqkv[:, 2 * D:], wv).then_inc(S["par_in"], 16)
            sp.dma_start(w2raw[:, 0:D], w_self).then_inc(S["par_in"], 16)
            sp.dma_start(w2raw[:, D:], w_neigh).then_inc(S["par_in"], 16)
            sp.dma_start(bias2[:, 0:D], b_self.rearrange("(o f) -> o f", o=1)).then_inc(S["par_in"], 16)
            sp.dma_start(bias2[:, D:], b_neigh.rearrange("(o f) -> o f", o=1)).then_inc(S["par_in"], 16)
            sp.dma_start(psw[:, :], ps_w.rearrange("o f -> (o f)").partition_broadcast(P)).then_inc(S["par_in"], 16)
            sp.wait_ge(S["blank_ready"], 1)
            sp.dma_start(w_table.rearrange("(r q) c -> r (q c)", r=L), blank).then_inc(S["w_cleared"], 16)
            ea_v = edge_attr.rearrange("(p j) f -> p (j f)", p=P)
            way = path(sp)

            def load_rows(p, tables):
                sp.sem_inc(S[p + "_ohT"], 1)

                def body(d, par, use, front, back):
                    if front:
                        sp.wait_ge(S[p + "_ohT"], d + 1)
                        for e, tab in enumerate(tables):
                            sp.dma_start(rowbc[:, e], slot_rows[tab, bass.ds(d * (C * L), C * L)].partition_broadcast(P)
                                         ).then_inc(S[p + "_row"], 16)
                tile_steps(sp, LAG[p], body)

            with sp.If(way < 1):
                sp.wait_ge(S["rowT_ready"], 6)
                for e in range(3):
                    full = Q // L
                    sp.dma_start(slot_rows[e, 0:full * L * L].rearrange("(c q r) -> q c r", q=L, r=L),
                                 rowT[:, e, 0:full, :]).then_inc(S["rows_out"], 16)
                    sp.dma_start(slot_rows[e, full * L * L:Q * L].rearrange("(q r) -> q r", r=L),
                                 rowT[0:Q - full * L, e, full, :]).then_inc(S["rows_out"], 16)
                sp.wait_ge(S["ln0_done"], 1)
                for c in range(J // CJ):
                    if c:
                        sp.wait_ge(S["ea_used"], c)
                    sp.dma_start(xs[:, :, :].rearrange("p t f -> p (t f)"), ea_v[:, c * CJ * D:(c + 1) * CJ * D]).then_inc(S["ea_in"], 16)
                sp.wait_ge(S["ea_used"], J // CJ)
                sp.dma_start(xs[:, :, :], x.rearrange("(t p) f -> p t f", p=P)).then_inc(S["x_back"], 16)
            with sp.Else():
                sp.dma_start(g_src, src.rearrange("(p j) -> p j", p=P)).then_inc(S["g_in"], 16)
                sp.dma_start(g_dst, dst.rearrange("(p j) -> p j", p=P)).then_inc(S["g_in"], 16)
                sp.dma_start(g_w, edge_weight.rearrange("(p j) -> p j", p=P)).then_inc(S["g_in"], 16)
                for c in range(J // CJ):
                    if c >= 2:
                        sp.wait_ge(S["g_ea_used"], c - 1)
                    sp.dma_start(ea[:, c % 2], ea_v[:, c * CJ * D:(c + 1) * CJ * D]).then_inc(S[f"g_ea_in{c % 2}"], 16)
                for n in range(K0):
                    sp.wait_ge(S["table_ready"], n + 1)
                    sp.dma_start(g_table.rearrange("(t p) f -> p t f", p=P), h[:, :, :]).then_inc(S["table_in"], 16)
            with sp.If(way < 1):
                sp.wait_ge(S["rows_out"], 96)
                sp.wait_ge(S["l0_done"], 1)
                load_rows("l1", (1, 2))
            with sp.Else():
                sp.wait_ge(S["table_ready"], K0 + 1)
                sp.dma_start(kv_table.rearrange("(t p) f -> p t f", p=P), kvs[:, :, D:]).then_inc(S["table_in"], 16)
                sp.dma_start(g_table.rearrange("(t p) f -> p t f", p=P), kvs[:, :, 0:D]).then_inc(S["table_in"], 16)
            with sp.If(way < 1):
                sp.wait_ge(S["w_placed"], 1)
                sp.wait_ge(S["l1_done"], 1)
                sp.dma_start(wsl, w_table.rearrange("(r q) c -> r q c", r=L)).then_inc(S["wsl_in"], 16)
                load_rows("l2", (0,))
            with sp.Else():
                sp.wait_ge(S["table_ready"], K0 + 2)
                sp.dma_start(g_table.rearrange("(t p) f -> p t f", p=P), h[:, :, :]).then_inc(S["table_in"], 16)
            with sp.If(way < 1):
                sp.wait_ge(S["l3_go"], 1)
                sp.dma_start(wsl, w_table.rearrange("(r q) c -> r q c", r=L)).then_inc(S["wsl_in"], 16)
                load_rows("l3", (0,))
            with sp.Else():
                sp.wait_ge(S["table_ready"], K0 + 3)
                sp.dma_start(g_table.rearrange("(t p) f -> p t f", p=P), h[:, :, :]).then_inc(S["table_in"], 16)
            sp.wait_ge(S["out_ready"], 1)
            sp.dma_start(out.rearrange("(t p) f -> p t f", p=P), xs[:, :, :]).then_inc(S["out_in"], 16)
            sp.wait_ge(S["out_in"], 16)

        @block.gpsimd
        def _(pool):
            pool.iota(iota_i, pattern=[[1, Q]], base=0, channel_multiplier=0).then_inc(S["pool_step"], 1)
            pool.iota(lane_i[:, :], pattern=[[0, 1]], base=0, channel_multiplier=1).then_inc(S["pool_step"], 1)
            pool.memset(ones[:, :], 1.0).then_inc(S["pool_step"], 1)
            pool.memset(ones_b[:, :], 1.0).then_inc(S["pool_step"], 1)
            pool.memset(zero_c, 0.0).then_inc(S["pool_step"], 1)
            pool.memset(earlier, 1.0).then_inc(S["pool_step"], 1)
            pool.memset(ident[:, :], 0.0).then_inc(S["pool_step"], 1)
            pool.memset(pair[:, :], 0.0).then_inc(S["pool_step"], 1)
            pool.wait_ge(S["pool_step"], 8)
            pool.affine_select(out=ident[:, :], in_=ident[:, :], compare_op=ALU.not_equal, fill=1.0,
                               base=0, pattern=[[-1, L]], channel_multiplier=1).then_inc(S["pool_step"], 1)
            pool.affine_select(out=earlier, in_=earlier, compare_op=ALU.is_ge, fill=0.0,
                               base=-1, pattern=[[1, P]], channel_multiplier=-1).then_inc(S["pool_step"], 1)
            pool.affine_select(out=pair[:, :], in_=pair[:, :], compare_op=ALU.not_equal, fill=1.0,
                               base=0, pattern=[[-1, D]], channel_multiplier=1).then_inc(S["pool_step"], 1)
            pool.wait_ge(S["pool_step"], 11)
            pool.affine_select(out=pair[:, :], in_=pair[:, :], compare_op=ALU.not_equal, fill=1.0,
                               base=-D, pattern=[[-1, D]], channel_multiplier=1).then_inc(S["pool_step"], 1)
            pool.memset(blank, 0.0).then_inc(S["blank_ready"], 1)
            way = path(pool)

            def gathers(n, p):
                k = 2 if p == "l1" else 1
                pool.wait_ge(S["table_in"], 16 * (n - 1 + k))
                with pool.Fori(0, J) as j:
                    pool.wait_ge(S["idx_ready"], n * J + 1 + j)
                    pool.sem_inc(S["gather_turn"], 1)
                    if p == "l1":
                        pool.indirect_dma_start(rows, None, kv_table, bass.IndirectOffsetOnAxis(idx_s, 0)).then_inc(S[f"gathered{n}"], 16)
                        pool.indirect_dma_start(rows_q, None, g_table, bass.IndirectOffsetOnAxis(idx_d, 0)).then_inc(S[f"gathered{n}"], 16)
                    else:
                        pool.indirect_dma_start(rows[:, 0:D], None, g_table, bass.IndirectOffsetOnAxis(idx_s, 0)).then_inc(S[f"gathered{n}"], 16)

            with pool.If(way < 1):
                halves = [0]
                pool.wait_ge(S["par_in"], 160)
                for c in range(J // CJ):
                    pool.wait_ge(S["ea_in"], 16 * (c + 1))
                    pool.tensor_tensor(xs[:, :, :], xs[:, :, :], psw[:, :].unsqueeze(1).to_broadcast([P, CJ, D]), ALU.mult).then_inc(S["ea_mult"], 1)
                    pool.wait_ge(S["ea_mult"], c + 1)
                    w = D
                    while w > 1:
                        w //= 2
                        last = pool.tensor_tensor(xs[:, :, 0:w], xs[:, :, 0:w], xs[:, :, w:2 * w], ALU.add)
                        last.then_inc(S["ea_half"], 1)
                        halves[0] += 1
                        pool.wait_ge(S["ea_half"], halves[0])
                    pool.tensor_copy(wpa[:, c * CJ:(c + 1) * CJ, 1], xs[:, :, 0]).then_inc(S["ea_used"], 1)
                pool.wait_ge(S["pa_ready"], 1)
                pool.wait_ge(S["w_cleared"], 16)

                def place_weights(i, u, again):
                    if again:
                        pool.wait_ge(S[f"w_out{u}"], i * 16)
                        pool.sem_inc(S["place_turn"], 1)
                    pool.tensor_copy(s_idx[:, u], slot_i[:, bass.ds(i * SU + u, 1)]).then_inc(S[f"w_copied{u}"], 1)
                    pool.tensor_copy(s_val[:, u], wpa[:, bass.ds(i * SU + u, 1), :]).then_inc(S[f"w_copied{u}"], 1)
                    pool.wait_ge(S[f"w_copied{u}"], i * 2 + 2)
                    pool.sem_inc(S["place_turn"], 1)
                    pool.indirect_dma_start(w_table, bass.IndirectOffsetOnAxis(s_idx[:, u], 0), s_val[:, u], None).then_inc(S[f"w_out{u}"], 16)
                for u in range(SU):
                    place_weights(0, u, False)
                with pool.Fori(1, J // SU) as i:
                    for u in range(SU):
                        place_weights(i, u, True)
                for u in range(SU):
                    pool.wait_ge(S[f"w_out{u}"], 16 * (J // SU))
                pool.sem_inc(S["w_placed"], 1)
            with pool.Else():
                pool.wait_ge(S["g_src_free"], 1)
                pool.iota(node_i, pattern=[[1, N]], base=0, channel_multiplier=0).then_inc(S["g_pool"], 1)
                pool.memset(zeros, 0.0).then_inc(S["g_pool"], 1)
                for n in range(K0):
                    gathers(n + 1, "l0")
                gathers(K0 + 1, "l1")
                gathers(K0 + 2, "l2")
                gathers(K0 + 3, "l3")

        @block.scalar
        def _(act):
            def std_of_var(n):
                act.wait_ge(S["var_ready"], n)
                act.activation(std[:, :], var[:, :], ACT.Sqrt).then_inc(S["std_ready"], 1)

            def edge_layer(p):
                groups, lag = GROUPS[p], LAG[p]
                ng = len(groups)
                G, w = (G1, 3 * D) if p == "l1" else (G2, D)
                m1 = M1 if p == "l1" else D
                act.sem_inc(S[p + "_rows"], ng)
                act.sem_inc(S[p + "_sums"], 2)

                def body(d, par, use, front, back):
                    if front:
                        c = 0
                        for m, n in enumerate(groups):
                            act.wait_ge(S[p + "_gath"], d * ng + (2 * ng + m + 1))
                            if m == 0:
                                act.wait_ge(S[p + ("_msg" if p == "l1" else "_scat")], d + 1)
                            act.activation(G[:, par, c:c + n, :], ps[:, m % RING, 0:n * w].rearrange("p (c f) -> p c f", c=n),
                                           ACT.Copy).then_inc(S[p + "_rows"], 1)
                            c += n
                    if p == "l1":
                        if (front and back) or (front and not isinstance(d, int)) or (isinstance(d, int) and 1 <= d <= T):
                            act.wait_ge(S["l1_logit"], d)
                            act.activation(msg1[:, 1 - par, :, D:M1], logit, ACT.Exp).then_inc(S["l1_exp"], 1)
                    if back:
                        q = d - lag
                        bank = RING + (par + lag) % 2
                        act.wait_ge(S[p + "_scat"], q + 3)
                        act.activation(agg[:, bass.ds(q, 1), 0:m1], ps[0:P, bank, 0:m1].unsqueeze(1), ACT.Copy).then_inc(S[p + "_sums"], 1)
                tile_steps(act, lag, body)

            way = path(act)
            std_of_var(1)
            with act.If(way < 1):
                for e in range(3):
                    for hlf in range(2):
                        act.wait_ge(S["rowT_ps"], 2 * e + hlf + 1)
                        n = min(4, QT - 4 * hlf)
                        for c in range(4 * hlf, 4 * hlf + n):
                            k = min(L, Q - c * L)
                            last = act.activation(rowT[0:k, e, c, :], ps[0:k, 2 + 2 * e + hlf, (c % 4) * L:(c % 4 + 1) * L], ACT.Copy)
                        last.then_inc(S["rowT_ready"], 1)
                act.sem_inc(S["adj_taken"], 6)
                with act.Fori(0, T) as d:
                    for g in range(6):
                        act.wait_ge(S["adj_mm"], d * 7 + (g + 8))
                        act.activation(adj[:, 4 * g:4 * g + 4, bass.ds(d * P, P)],
                                       ps[0:P, g, 0:4 * P].rearrange("p (s d) -> p s d", s=4), ACT.Copy).then_inc(S["adj_taken"], 1)
            std_of_var(2)
            with act.If(way < 1):
                act.sem_inc(S["mains_taken"], NCH)

                def chunks(i):
                    for u in range(2):
                        for c in range(NCH):
                            n = u * NCH + c
                            act.wait_ge(S["mains"], i * (2 * NCH) + (n + 1))
                            act.wait_ge(S["combined"], i * (2 * NCH) + (n + 1))
                            w = min(CH, T - CH * c) * P
                            act.activation(part[:, n % 2, 0:w], ps[:, c, 0:w], ACT.Copy).then_inc(S["mains_taken"], 1)
                act.wait_ge(S["rows_out"], 96)
                with act.Fori(0, 2) as i:
                    chunks(i)
                act.wait_ge(S["ea_used"], J // CJ)
                act.activation(wpa[:, :, 1], wpa[:, :, 1], ACT.Sigmoid).then_inc(S["pa_ready"], 1)
                with act.Fori(2, K0 // 2) as i:
                    chunks(i)
            with act.Else():
                act.wait_ge(S["g_z_ready"], 1)
                act.activation(g_pa, g_z, ACT.Sigmoid).then_inc(S["g_pa_ready"], 1)
            std_of_var(3)
            with act.If(way < 1):
                edge_layer("l1")
            with act.Else():
                with act.Fori(0, J) as j:
                    act.wait_ge(S["logit_ready"], j + 1)
                    act.activation(msg[:, D:M1], att2, ACT.Exp).then_inc(S["expd"], 1)
            std_of_var(4)
            with act.If(way < 1):
                edge_layer("l2")
            std_of_var(5)
            with act.If(way < 1):
                edge_layer("l3")

        @block.vector
        def _(vec):
            steps = [0]

            def step(ins):
                steps[0] += 1
                ins.then_inc(S["vec_step"], 1)
                vec.wait_ge(S["vec_step"], steps[0])

            class Chain:
                def __init__(self, name):
                    self.name, self.n = name, 0

                def __call__(self, ins, at=None):
                    self.n += 1
                    ins.then_inc(S[self.name], 1)
                    vec.wait_ge(S[self.name], self.n if at is None else at + self.n)

            def per_node(v):
                return v[:, :].unsqueeze(2).to_broadcast([P, T, D])

            n_norms = [0]

            def std_from_act():
                n_norms[0] += 1
                vec.wait_ge(S["std_ready"], n_norms[0])

            def layer_norm():
                step(vec.tensor_reduce(mean[:, :], xs[:, :, :], AX.X, ALU.add))
                step(vec.tensor_scalar(mean[:, :], mean[:, :], 1.0 / D, None, ALU.mult))
                step(vec.tensor_tensor(h[:, :, :], xs[:, :, :], per_node(mean), ALU.subtract))
                step(vec.tensor_tensor(base[:, :, :], h[:, :, :], h[:, :, :], ALU.mult))
                step(vec.tensor_reduce(var[:, :], base[:, :, :], AX.X, ALU.add))
                vec.tensor_scalar(var[:, :], var[:, :], 1.0 / D, EPS, ALU.mult, ALU.add).then_inc(S["var_ready"], 1)
                std_from_act()
                step(vec.reciprocal(rstd[:, :], std[:, :]))
                step(vec.tensor_tensor(h[:, :, :], h[:, :, :], per_node(rstd), ALU.mult))
                step(vec.tensor_scalar(h[:, :, :], h[:, :, :], 0.0, None, ALU.max))

            taken, chained = [0], [0]

            def gather_aggregate(p):
                n = taken[0]
                b = n * J
                k = 32 if p == "l1" else 16
                with vec.Fori(0, J) as j:
                    vec.wait_ge(S["scattered"], b + j + 1)
                    here, there, here_f = (g_src, g_dst, g_srcf) if p == "l1" else (g_dst, g_src, g_dstf)
                    vec.tensor_copy(idx_d, here[:, bass.ds(j, 1)])
                    vec.tensor_copy(idx_s, there[:, bass.ds(j, 1)]).then_inc(S["idx_ready"], 1)
                    vec.tensor_scalar(hit, node_f, here_f[:, bass.ds(j, 1)], None, ALU.is_equal).then_inc(S["hit_ready"], 1)
                    if p == "deg":
                        vec.memset(msg[:, 0:1], 1.0).then_inc(S["msg_ready"], 1)
                    else:
                        vec.wait_ge(S[f"gathered{n}"], k + j * k)
                    if p == "l0":
                        vec.tensor_copy(msg[:, 0:D], rows[:, 0:D]).then_inc(S["msg_ready"], 1)
                    if p == "l2":
                        vec.tensor_scalar(msg[:, 0:D], rows[:, 0:D], g_w[:, bass.ds(j, 1)], None, ALU.mult).then_inc(S["msg_ready"], 1)
                    if p == "l3":
                        vec.tensor_scalar(msg[:, 0:D], rows[:, 0:D], g_pa[:, bass.ds(j, 1)], None, ALU.mult).then_inc(S["msg_ready"], 1)
                    if p == "l1":
                        vec.tensor_tensor(qk, rows[:, 0:D], rows_q, ALU.mult).then_inc(S["qk_step"], 1)
                        vec.wait_ge(S["qk_step"], j * 2 + 1)
                        vec.tensor_reduce(att, qk.rearrange("p (a d) -> p a d", a=HEADS), AX.X, ALU.add).then_inc(S["qk_step"], 1)
                        vec.wait_ge(S["qk_step"], j * 2 + 2)
                        vec.tensor_scalar(att2, att, -10.0, 10.0, ALU.max, ALU.min).then_inc(S["logit_ready"], 1)
                        vec.wait_ge(S["expd"], j + 1)
                        vec.tensor_tensor(msg[:, 0:D].rearrange("p (a d) -> p a d", a=HEADS),
                                          rows[:, D:].rearrange("p (a d) -> p a d", a=HEADS),
                                          msg[:, D:M1].unsqueeze(2).to_broadcast([P, HEADS, HD]), ALU.mult).then_inc(S["msg_ready"], 1)
                taken[0] += 1
                vec.wait_ge(S["scattered"], taken[0] * J + 1)
                for q in range(NBANK):
                    last = vec.tensor_copy(agg[:, q * TB:(q + 1) * TB, :],
                                           acc[0:P, q, 0:TB * M1].rearrange("p (t f) -> p t f", t=TB))
                last.then_inc(S["acc_taken"], 1)
                vec.wait_ge(S["acc_taken"], taken[0])

            pts = [0]

            def take(dest_of, n):
                for i in range(n):
                    pts[0] += 1
                    vec.wait_ge(S["pt_ready"], pts[0])
                    dst_ap, src_ap = dest_of(i, (pts[0] - 1) % 2)
                    vec.tensor_copy(dst_ap, src_ap).then_inc(S["pt_taken"], 1)
                vec.wait_ge(S["pt_taken"], pts[0])

            def split3(x_ap, r_ap, p_of, chain):
                chain(vec.tensor_copy(p_of(0), x_ap))
                chain(vec.tensor_tensor(r_ap, x_ap, p_of(0), ALU.subtract))
                chain(vec.tensor_copy(p_of(1), r_ap))
                chain(vec.tensor_tensor(r_ap, r_ap, p_of(1), ALU.subtract))
                chain(vec.tensor_copy(p_of(2), r_ap))

            def edge_layer(p):
                lag = LAG[p]
                ng = len(GROUPS[p])
                ends = 2 if p == "l1" else 1
                vec.sem_inc(S[p + "_cols"], 1)
                if p == "l1":
                    vec.sem_inc(S["l1_msg"], 2)

                def onehots_T(d, par, use):
                    vec.wait_ge(S[p + "_row"], (d + 1) * (16 * ends))
                    vec.wait_ge(S[p + "_gath"], d * ng + ng)
                    for e in range(ends):
                        last = vec.tensor_scalar(ohT[:, par, e], rowbc[:, e], lane[0:P, :], None, ALU.is_equal)
                    last.then_inc(S[p + "_ohT"], 1)

                def onehots(d, par):
                    if p == "l1":
                        by_tile = sl[:, :].rearrange("p (d c) -> p c d", c=C)
                        vec.tensor_copy(cols[:, par, 0, 0:T], by_tile[:, bass.ds(d, 1), :].rearrange("p c d -> p (c d)"))
                        last = vec.tensor_copy(cols[:, par, 0, T:C], sl[:, bass.ds(d * C + T, 1)])
                    else:
                        vec.tensor_copy(cols[:, par, 0, :], dl[:, bass.ds(d * C, C)]).then_inc(S[p + "_cols"], 1)
                        wc = 0 if p == "l2" else 1
                        last = vec.tensor_copy(cols[:, par, 1, :], wsl[:, bass.ds(d * C, C), wc])
                    last.then_inc(S[p + "_cols"], 1)
                    vec.wait_ge(S[p + "_cols"], (d + 1) * (1 if p == "l1" else 2) + 1)
                    vec.wait_ge(S[p + "_scat"], d + 1)
                    for k in range(C):
                        last = vec.tensor_scalar(ohd[:, par, k, :], iota_f[:, :], cols[:, par, 0, k:k + 1],
                                                 None if p == "l1" else cols[:, par, 1, k:k + 1], ALU.is_equal,
                                                 ALU.bypass if p == "l1" else ALU.mult)
                    last.then_inc(S[p + "_ohd"], 1)

                def messages(q, par):
                    vec.wait_ge(S["l1_rows"], q * ng + 2 * ng)
                    vec.tensor_tensor(prod, G1[:, par, :, 0:D], G1[:, par, :, 2 * D:], ALU.mult).then_inc(S["l1_step"], 1)
                    vec.wait_ge(S["l1_step"], q * 2 + 1)
                    vec.tensor_reduce(logit.rearrange("p c a -> p (c a)"),
                                      prod.rearrange("p c (a d) -> p (c a) d", a=HEADS), AX.X, ALU.add).then_inc(S["l1_step"], 1)
                    vec.wait_ge(S["l1_step"], q * 2 + 2)
                    vec.wait_ge(S["l1_scat"], q + 1)
                    vec.tensor_scalar(logit, logit, -10.0, 10.0, ALU.max, ALU.min).then_inc(S["l1_logit"], 1)
                    vec.wait_ge(S["l1_exp"], q + 1)
                    vec.tensor_tensor(msg1[:, par, :, 0:D].rearrange("p c (a d) -> p c a d", a=HEADS),
                                      G1[:, par, :, D:2 * D].rearrange("p c (a d) -> p c a d", a=HEADS),
                                      msg1[:, par, :, D:M1].unsqueeze(3).to_broadcast([L, C, HEADS, HD]), ALU.mult
                                      ).then_inc(S["l1_msg"], 1)

                def body(d, par, use, front, back):
                    if front:
                        onehots_T(d, par, use)
                    if p == "l1" and not (isinstance(d, int) and (d == 0 or d > T)):
                        messages(d - 1, 1 - par)
                    if front:
                        onehots(d, par)
                tile_steps(vec, lag, body)
                vec.wait_ge(S[p + "_sums"], T + 2)

            vec.wait_ge(S["idx_in"], 32)
            vec.tensor_copy(src_f, src_i)
            step(vec.tensor_copy(dst_f, dst_i))
            for f, tile, ln in ((src_f, st, s_l), (dst_f, dt_, d_l)):
                step(vec.tensor_scalar(tile, f, -float(P // 2), 1.0 / P, ALU.add, ALU.mult))
                step(vec.tensor_scalar(tile, tile, ROUND, -ROUND, ALU.add, ALU.add))
                step(vec.scalar_tensor_tensor(ln, tile, -float(P), f, ALU.mult, ALU.add))
            vec.memset(same[:, 0:1], 1.0)
            vec.tensor_tensor(same[:, 1:J], dt_[:, 1:J], dt_[:, 0:J - 1], ALU.is_equal)
            step(vec.tensor_scalar(last_run, dt_, dt_[:, J - 1:J], None, ALU.is_equal))
            for s in range(T):
                last = vec.tensor_scalar(hits[:, s, :], st, float(s), None, ALU.is_equal)
            step(last)
            step(vec.tensor_tensor(picked, hits, last_run.unsqueeze(1).to_broadcast([P, T, J]), ALU.mult))
            vec.tensor_reduce(run_end, picked, AX.X, ALU.add)
            vec.wait_ge(S["pool_step"], 12)
            vec.tensor_scalar(first_d, ident[0:P, 0:P], dt_[:, 0:1], None, ALU.mult).then_inc(S["first_d"], 1)
            vec.wait_ge(S["first_ps"], 1)
            step(vec.tensor_scalar(first_r, ps[0:P, 0, 0:P], dt_[:, J - 1:J], None, ALU.is_lt))
            step(vec.tensor_tensor(first_r, first_r, earlier, ALU.mult))
            vec.tensor_reduce(bad[:, 0:1], first_r, AX.X, ALU.add)
            step(vec.tensor_scalar(link_m, ps[0:P, 0, 0:P], dt_[:, J - 1:J], None, ALU.is_equal))
            vec.tensor_tensor(link_m, link_m, earlier, ALU.mult).then_inc(S["link_ready"], 1)
            vec.wait_ge(S["carry_ps"], 1)
            step(vec.tensor_copy(carry, ps[0:P, 1, 0:T]))
            for s in range(T):
                last = vec.tensor_tensor_scan(runs[:, s, :], same, hits[:, s, :], carry[:, s:s + 1], ALU.mult, ALU.add)
            step(last)
            step(vec.tensor_tensor(picked, hits, runs, ALU.mult))
            step(vec.tensor_reduce(rank, picked.rearrange("p s j -> p j s"), AX.X, ALU.add))
            step(vec.tensor_scalar(rank, rank, -1.0, None, ALU.add))
            vec.tensor_scalar(over, rank, float(L), None, ALU.is_ge)
            step(vec.tensor_tensor(tmp_j, dt_, st, ALU.not_equal))
            step(vec.tensor_tensor(tmp_j, tmp_j, over, ALU.mult))
            step(vec.tensor_reduce(bad[:, 1:2], tmp_j, AX.X, ALU.add))
            step(vec.tensor_scalar(tmp_j, rank, 2.0 * L, None, ALU.is_ge))
            step(vec.tensor_reduce(bad[:, 2:3], tmp_j, AX.X, ALU.add))
            step(vec.tensor_tensor(tmp_j[:, 1:J], dt_[:, 1:J], dt_[:, 0:J - 1], ALU.is_lt))
            step(vec.tensor_reduce(bad[:, 3:4], tmp_j[:, 1:J], AX.X, ALU.add))
            vec.tensor_reduce(run_end[:, 0:1], bad, AX.X, ALU.add).then_inc(S["bad_ready"], 1)
            vec.wait_ge(S["bad_ps"], 1)
            step(vec.tensor_scalar(flag[:, :], ps[0:1, 2, 0:1], 1.0, None, ALU.min))
            step(vec.tensor_scalar(tmp_j, st, -1.0, float(T), ALU.mult, ALU.add))
            step(vec.tensor_tensor(tmp_j, tmp_j, over, ALU.mult))
            step(vec.tensor_tensor(tmp_j, tmp_j, st, ALU.add))
            vec.scalar_tensor_tensor(place[:, :, 1], dt_, float(C), tmp_j, ALU.mult, ALU.add)
            step(vec.scalar_tensor_tensor(place[:, :, 0], over, -float(L), rank, ALU.mult, ALU.add))
            step(vec.scalar_tensor_tensor(tmp_j, place[:, :, 0], float(Q), place[:, :, 1], ALU.mult, ALU.add))
            step(vec.tensor_copy(slot_i[:, :], tmp_j))
            step(vec.scalar_tensor_tensor(tmp_j, s_l, 128.0, d_l, ALU.mult, ALU.add))
            step(vec.tensor_scalar(place[:, :, 2].bitcast(I32), tmp_j, 128.0, 65536.0, ALU.add, ALU.mult))
            vec.wait_ge(S["edge_in"], 16)
            vec.tensor_copy(wpa[:, :, 0], edge_w)
            vec.tensor_copy(lane[:, :], lane_i[:, :])
            vec.tensor_copy(iota_f[:, :], iota_i[:, 0:P])
            step(vec.tensor_copy(iota_h[:, :], iota_i))
            vec.wait_ge(S["w_cleared"], 16)
            vec.sem_inc(S["flag_ready"], 1)
            way = path(vec)

            vec.wait_ge(S["x_in"], 16)
            vec.wait_ge(S["par_in"], 160)
            layer_norm()
            vec.sem_inc(S["ln0_done"], 1)

            with vec.If(way < 1):
                vec.sem_inc(S["to_slot"], 1)
                with vec.Fori(0, J // PU) as i:
                    vec.wait_ge(S["to_slot"], i * PU + 1)
                    vec.tensor_copy(place_u, place[:, bass.ds(i * PU, PU), :]).then_inc(S["place_in"], 1)
                    vec.wait_ge(S["place_in"], i + 1)
                    for u in range(PU):
                        vec.wait_ge(S["sorted"], i * PU + (u + 1))
                        vec.tensor_scalar(to_lane[:, u % PR], iota_h[0:P, 0:L], place_u[:, u, 0:1], None, ALU.is_equal)
                        vec.tensor_scalar(to_col[:, u % PR], iota_h[0:P, :], place_u[:, u, 1:2], place_u[:, u, 2:3],
                                          ALU.is_equal, ALU.mult).then_inc(S["to_slot"], 1)
                vec.wait_ge(S["sorted"], J + PR)
                fast = Chain("fast_step")
                vec.tensor_copy(bits[:, 0:QH], ps[:, 0, 0:QH])
                fast(vec.tensor_copy(bits[:, QH:Q], ps[:, 1, 0:QH]))
                vec.tensor_scalar(bits_a, bits.bitcast(I32), 23, None, ALU.logical_shift_right)
                fast(vec.tensor_scalar(bits_b, bits.bitcast(I32), 16, 127, ALU.logical_shift_right, ALU.bitwise_and))
                vec.tensor_copy(sl[:, :], bits_a)
                fast(vec.tensor_copy(dl[:, :], bits_b))
                fast(vec.tensor_scalar(sl[:, :], sl[:, :], -1.0, None, ALU.add))
                fast(vec.tensor_scalar(bits, sl[:, :], -1.0, None, ALU.is_equal))
                fast(vec.tensor_tensor(dl[:, :], dl[:, :], bits, ALU.subtract))
                for tab, tab_s in ((sl, sl_s), (dl, dl_s)):
                    by_tile = tab[:, :].rearrange("p (d c) -> p c d", c=C)
                    vec.tensor_copy(tab_s[:, :, 0:T], by_tile[:, 0:T, :])
                    fast(vec.tensor_copy(tab_s[:, :, T], by_tile[:, T, :]))
                vec.sem_inc(S["slots_ready"], 1)
                vec.sem_inc(S["adj_oh"], 1)
                with vec.Fori(0, T) as d:
                    vec.wait_ge(S["adj_oh"], d * 7 + 1)
                    vec.tensor_copy(cols[:, 0, 0, :], sl[:, bass.ds(d * C, C)])
                    vec.tensor_copy(cols[:, 0, 1, :], dl[:, bass.ds(d * C, C)]).then_inc(S["adj_cols"], 1)
                    vec.wait_ge(S["adj_cols"], d + 1)
                    k = 0
                    for g, n in enumerate(AG):
                        vec.wait_ge(S["adj_mm"], d * 7 + (g + 1))
                        for j in range(n):
                            for e in range(2):
                                o = late[:, e, j, :] if g == 6 else adj_oh[:, e, k, :]
                                last = vec.tensor_scalar(o, iota_h[:, 0:P], cols[:, 0, e, k:k + 1], None, ALU.is_equal)
                            k += 1
                        last.then_inc(S["adj_oh"], 1)
                    vec.wait_ge(S["adj_mm"], d * 7 + 14)
                    vec.tensor_copy(adj[:, T - 1, bass.ds(d * P, P)], ps[0:P, 6, 0:P]).then_inc(S["adj_last"], 1)
                    vec.tensor_copy(deg[:, bass.ds(d, 1)], ps[0:P, 7, 0:1])
                    vec.wait_ge(S["adj_last"], d + 1)
                    vec.wait_ge(S["adj_taken"], d * 6 + 12)
                    here = adj[:, bass.ds(d, 1), bass.ds(d * P, P)].rearrange("p s d -> p (s d)")
                    vec.tensor_tensor(here, here, ps[0:P, 6, P:2 * P], ALU.add).then_inc(S["adj_done"], 1)
                vec.wait_ge(S["adj_done"], T + 1)
                fast(vec.tensor_scalar(deg[:, :], deg[:, :], 1.0, None, ALU.max))
            with vec.Else():
                gen = Chain("gen_step")
                vec.sem_inc(S["g_src_free"], 1)
                vec.sem_inc(S["scattered"], 1)
                vec.wait_ge(S["g_in"], 48)
                vec.tensor_copy(g_dstf, g_dst)
                vec.tensor_copy(g_srcf, g_src)
                vec.wait_ge(S["g_pool"], 2)
                gen(vec.tensor_copy(node_f, node_i))
                for c in range(J // CJ):
                    vec.wait_ge(S[f"g_ea_in{c % 2}"], 16 * (c // 2 + 1))
                    ea_c = ea[:, c % 2].rearrange("p (j f) -> p j f", j=CJ)
                    gen(vec.tensor_tensor(ea_c, ea_c, psw[:, :].unsqueeze(1).to_broadcast([P, CJ, D]), ALU.mult))
                    vec.tensor_reduce(g_z[:, c * CJ:(c + 1) * CJ], ea_c, AX.X, ALU.add).then_inc(S["g_ea_used"], 1)
                vec.wait_ge(S["g_ea_used"], J // CJ)
                vec.sem_inc(S["g_z_ready"], 1)
                gather_aggregate("deg")
                gen(vec.tensor_scalar(deg[:, :], agg[:, 0:T, 0], 1.0, None, ALU.max))
            vec.tensor_copy(var[:, :], deg[:, :]).then_inc(S["var_ready"], 1)
            std_from_act()
            vec.reciprocal(rdeg[:, :], deg[:, :])
            step(vec.reciprocal(norm[:, :], std[:, :]))
            step(vec.tensor_scalar(base[:, :, :], h[:, :, :], ALPHA, None, ALU.mult))

            with vec.If(way < 1):
                fast(vec.tensor_scalar(coef[:, :], norm[:, :], GSCALE, None, ALU.mult))
                vec.tensor_tensor(h[:, :, :], h[:, :, :], per_node(coef), ALU.mult)
                fast(vec.tensor_tensor(base[:, :, :], base[:, :, :], per_node(coef), ALU.mult))
                fast(vec.tensor_copy(hl[0:P, 0, :, 0:D], h[:, :, :]))
                fast(vec.tensor_tensor(hl[0:P, 0, :, D:], h[:, :, :], hl[0:P, 0, :, 0:D], ALU.subtract))
                fast(vec.tensor_scalar(coef[:, :], rdeg[:, :], 1 - ALPHA, None, ALU.mult))
                vec.sem_inc(S["hl_ready"], NCH)
                vec.sem_inc(S["sums_read"], 1)
                with vec.Fori(0, K0 // 2) as i:
                    for u in range(2):
                        for c in range(NCH):
                            n = u * NCH + c
                            k = min(CH, T - CH * c)
                            t = slice(CH * c, CH * c + k)
                            sums = ps[0:P, 7, 0:k * D].rearrange("p (t f) -> p t f", t=k)
                            vec.wait_ge(S["combined"], i * (2 * NCH) + (n + 3))
                            vec.tensor_tensor(h[:, t, :], sums, coef[:, t].unsqueeze(2).to_broadcast([P, k, D]), ALU.mult
                                              ).then_inc(S["sums_read"], 1)
                            vec.wait_ge(S["sums_read"], i * (2 * NCH) + (n + 2))
                            vec.tensor_tensor(h[:, t, :], h[:, t, :], base[:, t, :], ALU.add).then_inc(S["g_step"], 1)
                            vec.wait_ge(S["g_step"], i * (4 * NCH) + (2 * n + 1))
                            vec.tensor_copy(hl[0:P, 1 - u, t, 0:D], h[:, t, :]).then_inc(S["g_step"], 1)
                            vec.wait_ge(S["g_step"], i * (4 * NCH) + (2 * n + 2))
                            vec.tensor_tensor(hl[0:P, 1 - u, t, D:], h[:, t, :], hl[0:P, 1 - u, t, 0:D], ALU.subtract
                                              ).then_inc(S["hl_ready"], 1)
                vec.wait_ge(S["hl_ready"], (K0 + 1) * NCH)
                vec.sem_inc(S["l0_done"], 1)
                fast(vec.tensor_scalar(coef[:, :], std[:, :], 1.0 / GSCALE, None, ALU.mult))
                fast(vec.tensor_tensor(h[:, :, :], h[:, :, :], per_node(coef), ALU.mult))
                vec.wait_ge(S["x_back"], 16)
            with vec.Else():
                gen(vec.tensor_scalar(coef[:, :], norm[:, :], 1 - ALPHA, None, ALU.mult))
                for it in range(K0):
                    vec.tensor_tensor(h[:, :, :], h[:, :, :], per_node(norm), ALU.mult).then_inc(S["table_ready"], 1)
                    gather_aggregate("l0")
                    gen(vec.tensor_tensor(h[:, :, :], agg[:, 0:T, 0:D], per_node(coef), ALU.mult))
                    gen(vec.tensor_tensor(h[:, :, :], h[:, :, :], base[:, :, :], ALU.add))
            step(vec.tensor_tensor(xs[:, :, :], xs[:, :, :], h[:, :, :], ALU.add))

            layer_norm()
            vec.sem_inc(S["h_ready"], 1)
            take(lambda i, s: (hT[:, i, :], ps[0:D, s, 0:P]), T)
            take(lambda i, s: (kvs[:, i, :], ps[0:P, s, 0:3 * D]), T)
            with vec.If(way < 1):
                split3(kvs, resid.rearrange("p (t f) -> p t f", t=T), lambda i: parts[:, :, i, :], fast)
                vec.sem_inc(S["parts_ready"], 1)
                edge_layer("l1")
                vec.sem_inc(S["l1_done"], 1)
            with vec.Else():
                vec.sem_inc(S["table_ready"], 1)
                gather_aggregate("l1")
            step(vec.tensor_scalar(agg[:, 0:T, D:M1], agg[:, 0:T, D:M1], 1e-8, None, ALU.add))
            step(vec.reciprocal(agg[:, 0:T, D:M1], agg[:, 0:T, D:M1]))
            for a in range(HEADS):
                last = vec.tensor_tensor(h[:, :, a * HD:(a + 1) * HD], agg[:, 0:T, a * HD:(a + 1) * HD],
                                         agg[:, 0:T, D + a:D + a + 1].to_broadcast([P, T, HD]), ALU.mult)
            step(last)
            step(vec.tensor_tensor(xs[:, :, :], xs[:, :, :], h[:, :, :], ALU.add))

            layer_norm()
            with vec.If(way < 1):
                split3(h[:, :, :], base[:, :, :], lambda i: parts[:, :, i, 0:D], fast)
                vec.sem_inc(S["parts_ready"], 1)
                vec.wait_ge(S["wsl_in"], 16)
                edge_layer("l2")
            with vec.Else():
                vec.sem_inc(S["table_ready"], 1)
                gather_aggregate("l2")
            step(vec.tensor_tensor(base[:, :, :], agg[:, 0:T, 0:D], per_node(rdeg), ALU.mult))
            vec.sem_inc(S["h_ready"], 1)
            take(lambda i, s: (hT[:, i, :], ps[0:D, s, 0:P]), T)
            take(lambda i, s: (nT[:, i, :], ps[0:D, s, 0:P]), T)
            take(lambda i, s: (w2[:, i * D:(i + 1) * D], ps[0:D, s, 0:D]), 2)
            vec.sem_inc(S["w2_ready"], 1)
            take(lambda i, s: (h[:, i, :], ps[0:P, s, 0:D]), T)
            step(vec.tensor_tensor(xs[:, :, :], xs[:, :, :], h[:, :, :], ALU.add))
            vec.sem_inc(S["l3_go"], 1)

            layer_norm()
            step(vec.tensor_tensor(h[:, :, :], h[:, :, :], per_node(cjs), ALU.mult))
            with vec.If(way < 1):
                split3(h[:, :, :], base[:, :, :], lambda i: parts[:, :, i, 0:D], fast)
                vec.sem_inc(S["parts_ready"], 1)
                vec.wait_ge(S["wsl_in"], 32)
                edge_layer("l3")
            with vec.Else():
                vec.sem_inc(S["table_ready"], 1)
                gather_aggregate("l3")
            step(vec.tensor_tensor(h[:, :, :], agg[:, 0:T, 0:D], per_node(cis), ALU.mult))
            vec.tensor_tensor(xs[:, :, :], xs[:, :, :], h[:, :, :], ALU.add).then_inc(S["out_ready"], 1)

        @block.tensor
        def _(pe):
            passes, pts = [0], [0]

            def gather_aggregate(p):
                w = WIDTH[p]
                b = passes[0] * J
                if passes[0]:
                    pe.wait_ge(S["acc_taken"], passes[0])
                for q in range(NBANK):
                    pe.matmul(acc[0:P, q, :], zeros[:, 0:P], zeros, start=True, stop=True)
                with pe.Fori(0, J) as j:
                    pe.wait_ge(S["msg_ready"], b + 1 + j)
                    pe.wait_ge(S["hit_ready"], b + 1 + j)
                    for t in range(T):
                        last = pe.matmul(acc[0:P, t // TB, (t % TB) * M1:(t % TB) * M1 + w],
                                         hit[:, t * P:(t + 1) * P], msg[:, 0:w], start=False, stop=True,
                                         skip_group_check=True)
                    last.then_inc(S["scattered"], 1)
                passes[0] += 1

            def slot():
                s = pts[0] % 2
                if pts[0] >= 2:
                    pe.wait_ge(S["pt_taken"], pts[0] - 1)
                pts[0] += 1
                return s

            def transposes(src_of, n, k):
                for i in range(n):
                    s = slot()
                    pe.transpose(ps[0:D, s, 0:k], src_of(i), ident[0:k, 0:k]).then_inc(S["pt_ready"], 1)

            def edge_layer(p, n_parts):
                groups, lag = GROUPS[p], LAG[p]
                ng = len(groups)
                w = 3 * D if p == "l1" else D
                m1 = M1 if p == "l1" else D
                pe.sem_inc(S[p + "_gath"], 2 * ng)
                pe.sem_inc(S[p + "_scat"], 2)
                pe.wait_ge(S["parts_ready"], n_parts)

                def gather(d, par, m, c, n):
                    if m == 0:
                        pe.wait_ge(S[p + "_ohT"], d + 2)
                    prev = m - RING + 1 + ng if m >= RING else max(k for k in range(ng) if k % RING == m) + 1
                    pe.wait_ge(S[p + "_rows"], d * ng + prev)
                    for k in range(c, c + n):
                        o = (k - c) * w
                        lhs = ohT[:, par, 0, k * L:(k + 1) * L]
                        for i in range(3):
                            a, b = (D, 3 * D) if p == "l1" else (0, D)
                            rhs = parts[:, k, i, a:b] if k < T else \
                                parts[:, bass.ds(d, 1), i, a:b].rearrange("p t f -> p (t f)")
                            last = pe.matmul(ps[:, m % RING, o:o + b - a], lhs, rhs, start=(i == 0), stop=(i == 2))
                        if p == "l1":
                            for i in range(3):
                                rhs = parts[:, bass.ds(d, 1), i, 0:D].rearrange("p t f -> p (t f)")
                                last = pe.matmul(ps[:, m % RING, o + 2 * D:o + w], ohT[:, par, 1, k * L:(k + 1) * L], rhs,
                                                 start=(i == 0), stop=(i == 2))
                    last.then_inc(S[p + "_gath"], 1)

                def scatter(q, par, c, n):
                    bank = RING + par
                    if c == 0:
                        pe.wait_ge(S[p + "_ohd"], q + 1)
                        if p == "l1":
                            pe.wait_ge(S["l1_msg"], q + 3)
                        else:
                            pe.wait_ge(S[p + "_rows"], q * ng + 2 * ng)
                        pe.wait_ge(S[p + "_sums"], q + 1)
                    for k in range(c, c + n):
                        last = pe.matmul(ps[0:P, bank, 0:m1], ohd[:, par, k, :],
                                         msg1[:, par, k, :] if p == "l1" else G2[:, par, k, :],
                                         start=(k == 0), stop=(k == C - 1))
                    if c + n == C:
                        last.then_inc(S[p + "_scat"], 1)

                def body(d, par, use, front, back):
                    c = 0
                    for m, n in enumerate(groups):
                        if front:
                            gather(d, par, m, c, n)
                        if back:
                            scatter(d - lag, (par + lag) % 2, c, n)
                        c += n
                tile_steps(pe, lag, body)

            pe.wait_ge(S["pool_step"], 12)
            pe.wait_ge(S["first_d"], 1)
            pe.matmul(ps[0:P, 0, 0:P], ones[0:P, 0:P], first_d, start=True, stop=True).then_inc(S["first_ps"], 1)
            pe.wait_ge(S["link_ready"], 1)
            pe.matmul(ps[0:P, 1, 0:T], link_m, run_end, start=True, stop=True).then_inc(S["carry_ps"], 1)
            pe.wait_ge(S["bad_ready"], 1)
            pe.matmul(ps[0:1, 2, 0:1], run_end[:, 0:1], ones[0:P, 0:1], start=True, stop=True).then_inc(S["bad_ps"], 1)
            way = path(pe)

            with pe.If(way < 1):
                pe.sem_inc(S["sorted"], PR)
                for b in range(2):
                    pe.matmul(ps[:, b, 0:QH], zero_c[:, 0:L], zero_c[:, 0:QH], start=True, stop=True)
                with pe.Fori(0, J // PU) as i:
                    for u in range(PU):
                        pe.wait_ge(S["to_slot"], i * PU + (u + 2))
                        for b in range(2):
                            last = pe.matmul(ps[:, b, 0:QH], to_lane[:, u % PR], to_col[:, u % PR, b * QH:(b + 1) * QH],
                                             start=False, stop=True, skip_group_check=True)
                        last.then_inc(S["sorted"], 1)
                pe.wait_ge(S["slots_ready"], 1)
                for e, tab in enumerate((sl, dl_s.rearrange("p s c -> p (s c)"), sl_s.rearrange("p s c -> p (s c)"))):
                    for c in range(QT):
                        k = min(L, Q - c * L)
                        last = pe.transpose(ps[0:k, 2 + 2 * e + c // 4, (c % 4) * L:(c % 4 + 1) * L], tab[:, c * L:c * L + k], ident[:, :])
                        if c in (3, QT - 1):
                            last.then_inc(S["rowT_ps"], 1)
                pe.wait_ge(S["rowT_ready"], 6)
                pe.sem_inc(S["adj_mm"], 7)
                pe.sem_inc(S["adj_done"], 1)
                with pe.Fori(0, T) as d:
                    k = 0
                    pe.wait_ge(S["adj_done"], d + 1)
                    for g, n in enumerate(AG):
                        pe.wait_ge(S["adj_oh"], d * 7 + (g + 2))
                        if g < 6:
                            pe.wait_ge(S["adj_taken"], d * 6 + (g + 1))
                        for j in range(n):
                            a, b = (late[:, 0, j, :], late[:, 1, j, :]) if g == 6 else (adj_oh[:, 0, k, :], adj_oh[:, 1, k, :])
                            pe.matmul(ps[0:P, g, j * P:(j + 1) * P], a, b, start=True, stop=True)
                            last = pe.matmul(ps[0:P, 7, 0:1], b, ones_b[:, :], start=(k == 0), stop=(k == C - 1))
                            k += 1
                        last.then_inc(S["adj_mm"], 1)
                pe.sem_inc(S["combined"], 2)
                with pe.Fori(0, K0 // 2) as i:
                    def combine(n, c):
                        pe.wait_ge(S["mains_taken"], i * (2 * NCH) + (NCH + n + 1))
                        pe.wait_ge(S["sums_read"], i * (2 * NCH) + (n + 1))
                        for k in range(min(CH, T - CH * c)):
                            o = k * D
                            last = pe.matmul(ps[0:P, 7, o:o + D], part[:, n % 2, k * P:(k + 1) * P], pair[:, :], start=True, stop=True)
                        last.then_inc(S["combined"], 1)

                    for u in range(2):
                        for c in range(NCH):
                            n = u * NCH + c
                            w = min(CH, T - CH * c) * P
                            pe.wait_ge(S["mains_taken"], i * (2 * NCH) + (n + 1))
                            for s in range(T):
                                if c == 0 and s % CH == 0:
                                    pe.wait_ge(S["hl_ready"], i * (2 * NCH) + (u * NCH + s // CH + 1))
                                last = pe.matmul(ps[:, c, 0:w], hl[0:P, u, s, :], adj[:, s, c * CH * P:c * CH * P + w],
                                                 start=(s == 0), stop=(s == T - 1))
                            last.then_inc(S["mains"], 1)
                            if c:
                                combine(n - 1, c - 1)
                        combine(n, c)
            with pe.Else():
                pe.wait_ge(S["g_pool"], 2)
                gather_aggregate("deg")
                for _ in range(K0):
                    gather_aggregate("l0")
            pe.wait_ge(S["h_ready"], 1)
            transposes(lambda i: h[:, i, :], T, P)
            pe.wait_ge(S["pt_taken"], pts[0])
            for i in range(T):
                s = slot()
                pe.matmul(ps[0:P, s, 0:3 * D], hT[:, i, :], wqkv[:, :], start=True, stop=True).then_inc(S["pt_ready"], 1)
            with pe.If(way < 1):
                edge_layer("l1", 1)
                edge_layer("l2", 2)
            with pe.Else():
                gather_aggregate("l1")
                gather_aggregate("l2")
            pe.wait_ge(S["h_ready"], 2)
            transposes(lambda i: h[:, i, :], T, P)
            transposes(lambda i: base[:, i, :], T, P)
            transposes(lambda i: w2raw[:, i * D:(i + 1) * D], 2, D)
            pe.wait_ge(S["w2_ready"], 1)
            for i in range(T):
                s = slot()
                pe.matmul(ps[0:P, s, 0:D], hT[:, i, :], w2[:, 0:D], start=True, stop=False)
                pe.matmul(ps[0:P, s, 0:D], nT[:, i, :], w2[:, D:], start=False, stop=False)
                pe.matmul(ps[0:P, s, 0:D], ones[0:1, 0:P], bias2[:, 0:D], start=False, stop=False)
                pe.matmul(ps[0:P, s, 0:D], ones[0:1, 0:P], bias2[:, D:], start=False, stop=True).then_inc(S["pt_ready"], 1)
            with pe.If(way < 1):
                edge_layer("l3", 3)
            with pe.Else():
                gather_aggregate("l3")


_INS = ['x', 'src', 'dst', 'edge_attr_64', 'edge_weight', 'node_vec1', 'node_vec1_n2', 'L1_gnn_qTrans',
        'L1_gnn_kTrans', 'L1_gnn_vTrans', 'L2_gnn_W_self', 'L2_gnn_b_self', 'L2_gnn_W_neigh',
        'L2_gnn_b_neigh', 'L3_gnn_ps_w']


def kernel(**inputs):
    import numpy as _np
    import concourse.bacc as _bacc
    from concourse import mybir as _mybir
    from concourse.bass_utils import run_bass_kernel_spmd as _run

    nc = _bacc.Bacc("TRN2", target_bir_lowering=False, num_devices=1)
    arrays, args = {}, []
    for name in _INS:
        a = _np.ascontiguousarray(inputs[name])
        arrays[f"in_{name}_dram"] = a
        args.append(nc.dram_tensor(f"in_{name}_dram", a.shape, _mybir.dt.from_np(a.dtype), kind="ExternalInput").ap())
    args.append(nc.dram_tensor("out_dram", (N, D), F32, kind="ExternalOutput").ap())
    graph_net(nc, *args)
    r = _run(nc, [arrays], core_ids=[0])
    return r.results[0]["out_dram"]
```

```python
import concourse.bass as bass
from concourse import mybir
from contextlib import ExitStack

F32, F16, BF16, I32 = mybir.dt.float32, mybir.dt.float16, mybir.dt.bfloat16, mybir.dt.int32
SIZE = {F32: 4, I32: 4, F16: 2, BF16: 2}
ALU, ACT, AX = mybir.AluOpType, mybir.ActivationFunctionType, mybir.AxisListType

N, E, D = 3125, 53125, 64
P = 125
T = N // P
J = E // P
HEADS, HD = 4, D // 4
M1 = D + HEADS
TB = 7
NBANK = -(-T // TB)
K0, ALPHA, EPS = 10, 0.1, 1e-5
CJ = 25
ROUND = 12582912.0

L = 128
C = T + 1
Q = T * C
QT = -(-Q // L)
GSCALE = 4096.0
CH = 4
NCH = -(-T // CH)
JT = J // T
JP = JT + 1
BT = 5
W2 = 2 * C
JH = 9
TA = 14
AG = [4] * 6 + [2]
KG = [14, 12]
SU = 5


def graph_net(nc, x, src, dst, edge_attr, edge_weight, cj, ci,
              wq, wk, wv, w_self, b_self, w_neigh, b_neigh, ps_w, out):
    ctx = ExitStack()
    with ctx:
        def sb(name, shape, dt=F32):
            return ctx.enter_context(nc.sbuf_tensor(name, shape, dt))

        def sem(name):
            return ctx.enter_context(nc.semaphore(name))

        g_table = nc.dram_tensor("g_table", [N, D], F32).ap()
        kv_table = nc.dram_tensor("kv_table", [N, 2 * D], F32).ap()
        slot_rows = nc.dram_tensor("slot_rows", [3, Q * L], BF16).ap()
        w_table = nc.dram_tensor("w_table", [L * Q, 2], F32).ap()

        edge_place = nc.dram_tensor("edge_place", [E, 3], F32).ap()

        xs = sb("xs", [P, T, D])
        h_room = sb("h_room", [L, C * M1])
        h = h_room[0:P, 0:T * D].rearrange("p (t f) -> p t f", t=T)
        base_room = sb("base_room", [L, C * D])
        base = base_room[0:P, 0:T * D].rearrange("p (t f) -> p t f", t=T)
        hl_room = sb("hl_room", [L, 2 * KG[0] * P])
        part_room = sb("part_room", [L, 2 * Q])
        part = part_room[:, 0:2 * CH * P].rearrange("p (a n) -> p a n", a=2)
        sl_h = sb("sl_h", [L, Q], F16)
        dl_h = sb("dl_h", [L, Q], F16)
        sls_h = sb("sls_h", [L, Q], F16)
        slot_i = sb("slot_i", [P, J], I32)
        wpa = sb("wpa", [P, J, 2])
        mean = sb("mean", [P, T])
        var = sb("var", [P, T])
        std = sb("std", [P, T])
        rstd = sb("rstd", [P, T])
        deg = sb("deg", [P, T])
        norm = sb("norm", [P, T])
        rdeg = sb("rdeg", [P, T])
        coef = sb("coef", [P, T])
        cjs = sb("cjs", [P, T])
        cis = sb("cis", [P, T])
        wqkv = sb("wqkv", [D, 3 * D])
        w2raw = sb("w2raw", [D, 2 * D])
        w2 = sb("w2", [2 * D, D])
        bias2 = sb("bias2", [1, 2 * D])
        psw = sb("psw", [P, D])
        ident = sb("ident", [L, L])
        ones = sb("ones", [L, L])
        pair = sb("pair", [L, D])
        ones_b = sb("ones_b", [L, 1], BF16)
        lane_i = sb("lane_i", [L, 1], I32)
        lane = sb("lane", [L, 1])
        iota_h = sb("iota_h", [L, Q], F16)
        flag = sb("flag", [1, 1], I32)
        top = sb("top", [L, 3])
        top_r = sb("top_r", [L, 3])
        top_g = sb("top_g", [3, 4])
        top_cj = sb("top_cj", [L, 1])
        s_idx = sb("s_idx", [P, 2, SU], I32)
        s_val = sb("s_val", [P, 2, SU, 2])

        arena = sb("arena", [L, -(-T * N // 2)])

        class Carver:
            def __init__(self, at=0):
                self.at = at

            def __call__(self, shape, dt=F32):
                n = 1
                for d in shape[1:]:
                    n *= d
                words = -(-n * SIZE[dt] // 4)
                v = arena[0:shape[0], self.at:self.at + words]
                self.at += words
                assert self.at <= -(-T * N // 2)
                if dt != F32:
                    v = v.bitcast(dt)
                v = v[:, 0:n]
                if len(shape) == 3:
                    v = v.rearrange("p (a b) -> p a b", a=shape[1])
                if len(shape) == 4:
                    v = v.rearrange("p (a b c) -> p a b c", a=shape[1], b=shape[2])
                return v

        adj = arena[0:P, :].bitcast(F16)[:, 0:T * N].rearrange("p (s d) -> p s d", s=T)

        hl = hl_room[:, 0:2 * T * D].bitcast(F16).rearrange("p (a t f) -> p a t f", a=2, t=T)
        rowbc = hl_room[0:P, 0:C * L].bitcast(BF16).rearrange("p (e n) -> p e n", e=2)
        rowT = part_room[:, 0:3 * QT * L // 2].bitcast(BF16).rearrange("p (e c r) -> p e c r", e=3, c=QT)
        wsl = part_room[:, :].rearrange("p (q c) -> p q c", c=2)
        adj_oh = [[hl_room[:, (2 * g + e) * KG[0] * P // 2:(2 * g + e) * KG[0] * P // 2 + n * P // 2].bitcast(BF16)
                   .rearrange("p (r c) -> p r c", c=n) for e in range(2)] for g, n in enumerate(KG)]

        ea_in = hl_room[0:P, 0:2 * CJ * D].rearrange("p (b j f) -> p b j f", b=2, j=CJ)

        cv = Carver()
        src_i, dst_i = cv([P, J], I32), cv([P, J], I32)
        src_f, dst_f = cv([P, J]), cv([P, J])
        st, dt_ = cv([P, J]), cv([P, J])
        s_l, d_l = cv([P, J]), cv([P, J])
        same, last_run = cv([P, J], F16), cv([P, J], F16)
        hits = cv([P, T, J], F16)
        runs = cv([P, T, J], F16)
        picked = cv([P, T, J], F16)
        rank, over, tmp_j = cv([P, J]), cv([P, J]), cv([P, J])
        place = cv([P, J, 3])
        edge_i, first_t = cv([P, J], I32), cv([P, J])
        placed = cv([BT * JT, T // BT, P * 3])
        lane_c, col_c = cv([P, T, JP], F16), cv([P, T, JP], F16)
        load_i = cv([P, J], I32)
        load_c = cv([P, T, JP], BF16)
        rep_s = cv([P, L, JP], F16)
        iota_i = cv([L, Q], I32)
        edge_w = cv([P, J])
        blank = cv([L, 2 * Q])
        to_lane = cv([P, 2, L, JP], BF16)
        to_col = cv([P, 2, W2, JP], BF16)
        hit_col = cv([P, W2, JP], BF16)
        bits = cv([L, Q])
        bits_a, bits_b = cv([L, Q], I32), cv([L, Q], I32)
        sl, dl = cv([L, Q]), cv([L, Q])
        sl_s, dl_s = cv([L, T, C]), cv([L, T, C])
        carry, run_end = cv([P, T]), cv([P, T])
        first_d, first_r, earlier, link_m = cv([P, P]), cv([P, P]), cv([P, P]), cv([P, P])
        bad = cv([P, 5])
        zero_c = cv([P, 512])

        cv = Carver()
        agg = cv([P, NBANK * TB, M1])
        node_end = cv.at
        kvs = cv([P, T, 3 * D])
        hT = cv([D, T, P])
        cv = Carver(node_end)
        cat = cv([P, T, 2 * D])
        catT = cv([2 * D, T, P])

        cv = Carver(node_end + T * 3 * D + T * P)
        g_src, g_dst = cv([P, J], I32), cv([P, J], I32)
        g_srcf = cv([P, J])
        g_dstf, g_w, g_pa, g_z = cv([P, J]), cv([P, J]), cv([P, J]), cv([P, J])
        ea = cv([P, 2, CJ * D])
        node_i, node_f = cv([P, N], I32), cv([P, N])
        hit = cv([P, N])
        idx_s, idx_d = cv([P, 1], I32), cv([P, 1], I32)
        rows, rows_q = cv([P, 2 * D]), cv([P, D])
        qk, att, att2, msg = cv([P, D]), cv([P, HEADS]), cv([P, HEADS]), cv([P, M1])
        zeros = cv([P, 512])

        cv = Carver(arena.shape[1] - T * 3 * M1 - T * 3 * D - 8)
        edge_end = cv.at
        sums = cv([P, T, 3 * M1])
        parts = cv([P, T, 2, 3 * D], F16)
        cv = Carver()
        G1 = cv([L, 2, C, 3 * D])
        G1m = [cv([L, C, M1]), h_room[:, :].rearrange("p (c f) -> p c f", c=C)]
        logit = cv([L, C, HEADS])
        msg1 = cv([L, 2, C, 3 * M1], BF16)
        prod = base_room[:, :].rearrange("p (c f) -> p c f", c=C)
        ohT = cv([P, 2, 2, C * L], BF16)
        ohd = cv([L, 2, P, C], BF16)
        rep_i = cv([L, P, C], F16)
        assert cv.at <= edge_end
        cv = Carver()
        msgf = cv([L, 2, C, D])
        msg2 = cv([L, 2, C, 2 * D], F16)
        assert cv.at <= 2 * C * 3 * D
        adj_rep = base_room[:, 0:P * C // 2].bitcast(F16).rearrange("p (r c) -> p r c", c=C)

        ps = ctx.enter_context(nc.psum_tensor("ps", [L, 8, 512], F32))
        acc = ps[:, 2:2 + NBANK, :]

        class Sems(dict):
            def __missing__(self, name):
                self[name] = sem(name)
                return self[name]
        S = Sems()
        block = ctx.enter_context(nc.Block())
        PASSES = ["deg"] + ["l0"] * K0 + ["l1", "l2", "l3"]
        WIDTH = {"deg": 1, "l0": D, "l1": M1, "l2": D, "l3": D}
        GROUPS = {"l1": [2] * (C // 2), "l2": [7, 6, 6, 7], "l3": [7, 6, 6, 7]}
        RING = 6

        BANKS = [0, 1, 6, 7]
        PLAN = [(stage, owners[(a // per) % len(owners)], a, min(per, n - a))
                for stage, n, per, owners in (("l1_h", T, 4, "va"), ("l1_qkv", T, 2, "va"), ("l2_cat", T, 4, "va"),
                                              ("l2_w", 1, 1, "v"), ("l2_out", T, 8, "v"))
                for a in range(0, n, per)]

        def turn(g):
            return sum(p[1] == PLAN[g][1] for p in PLAN[:g + 1])

        def fill(stage, emit):
            for g, (name, owner, first, n) in enumerate(PLAN):
                if name == stage:
                    if g >= len(BANKS):
                        nc.tensor.wait_ge(S["taken_" + PLAN[g - len(BANKS)][1]], turn(g - len(BANKS)))
                    for k in range(n):
                        last = emit(first + k, k, n, BANKS[g % len(BANKS)])
                    last.then_inc(S["bank_full"], 1)

        def take(eng, me, stage, copy):
            for g, (name, owner, first, n) in enumerate(PLAN):
                if name == stage and owner == me:
                    eng.wait_ge(S["bank_full"], g + 1)
                    copy(first, n, BANKS[g % len(BANKS)]).then_inc(S["taken_" + me], 1)

        def all_taken(eng, stage):
            for g, (name, owner, first, n) in enumerate(PLAN):
                if name == stage and not any(p[0:2] == (stage, owner) for p in PLAN[g + 1:]):
                    eng.wait_ge(S["taken_" + owner], turn(g))

        def path(eng):
            eng.wait_ge(S["flag_ready"], 1)
            return eng.value_load(flag[0:1, 0:1], min_val=0, max_val=1)

        LAST = 4
        ROOMS = {"l1": 1, "l2": 2, "l3": 2}

        def tile_steps(eng, body):
            last = LAST
            for s in range(last):
                body(s, s % 2, [k for k in range(last + 1) if k <= s])
            start = last
            if (T - start) % 2:
                body(start, start % 2, range(last + 1))
                start += 1
            with eng.Fori(0, (T - start) // 2) as i:
                for u in range(2):
                    body(i * 2 + (start + u), (start + u) % 2, range(last + 1))
            for s in range(T, T + last):
                body(s, s % 2, [k for k in range(last + 1) if s - k < T])

        @block.sync
        def _(sp):
            sp.dma_start(src_i, src.rearrange("(p j) -> p j", p=P)).then_inc(S["idx_in"], 16)
            sp.dma_start(dst_i, dst.rearrange("(p j) -> p j", p=P)).then_inc(S["idx_in"], 16)
            sp.dma_start(xs[:, :, :], x.rearrange("(t p) f -> p t f", p=P)).then_inc(S["x_in"], 16)
            sp.dma_start(edge_w, edge_weight.rearrange("(p j) -> p j", p=P)).then_inc(S["edge_in"], 16)
            with nc.allow_non_contiguous_dma("node vectors of one column"):
                sp.dma_start(cjs[:, :], cj.rearrange("(t p) o -> p (t o)", p=P)).then_inc(S["par_in"], 16)
                sp.dma_start(cis[:, :], ci.rearrange("(t p) o -> p (t o)", p=P)).then_inc(S["par_in"], 16)
            sp.dma_start(wqkv[:, 0:D], wq).then_inc(S["par_in"], 16)
            sp.dma_start(wqkv[:, D:2 * D], wk).then_inc(S["par_in"], 16)
            sp.dma_start(wqkv[:, 2 * D:], wv).then_inc(S["par_in"], 16)
            sp.dma_start(w2raw[:, 0:D], w_self).then_inc(S["par_in"], 16)
            sp.dma_start(w2raw[:, D:], w_neigh).then_inc(S["par_in"], 16)
            sp.dma_start(bias2[:, 0:D], b_self.rearrange("(o f) -> o f", o=1)).then_inc(S["par_in"], 16)
            sp.dma_start(bias2[:, D:], b_neigh.rearrange("(o f) -> o f", o=1)).then_inc(S["par_in"], 16)
            sp.dma_start(psw[:, :], ps_w.rearrange("o f -> (o f)").partition_broadcast(P)).then_inc(S["par_in"], 16)
            sp.wait_ge(S["blank_ready"], 1)
            sp.dma_start(w_table.rearrange("(r q) c -> r (q c)", r=L), blank).then_inc(S["w_cleared"], 16)
            ea_v = edge_attr.rearrange("(p j) f -> p (j f)", p=P)
            for c in range(J // CJ):
                if c >= 2:
                    sp.wait_ge(S["ea_used"], c - 1)
                sp.dma_start(hl_room[0:P, (c % 2) * CJ * D:(c % 2 + 1) * CJ * D], ea_v[:, c * CJ * D:(c + 1) * CJ * D]
                             ).then_inc(S[f"ea_in{c % 2}"], 16)
            way = path(sp)

            def load_rows(p, tables):
                free = ROOMS[p]
                sp.sem_inc(S[p + "_ohT"], free)
                if p == "l1":
                    sp.sem_inc(S["l1_first"], 1)

                def body(d, par, on):
                    if 0 in on:
                        for e, tab in enumerate(tables):
                            room = e if p == "l1" else par
                            sp.wait_ge(S["l1_first" if p == "l1" and e == 0 else p + "_ohT"], d + 1)
                            sp.dma_start(rowbc[:, room], slot_rows[tab, bass.ds(d * (C * L), C * L)].partition_broadcast(P)
                                         ).then_inc(S[p + f"_row{room}"], 16)
                tile_steps(sp, body)
                sp.wait_ge(S[p + "_ohT"], T + free)

            with sp.If(way < 1):
                sp.wait_ge(S["rowT_ready"], 6)
                for e in range(3):
                    full = Q // L
                    sp.dma_start(slot_rows[e, 0:full * L * L].rearrange("(c q r) -> q c r", q=L, r=L),
                                 rowT[:, e, 0:full, :]).then_inc(S["rows_out"], 16)
                    sp.dma_start(slot_rows[e, full * L * L:Q * L].rearrange("(q r) -> q r", r=L),
                                 rowT[0:Q - full * L, e, full, :]).then_inc(S["rows_out"], 16)
            with sp.Else():
                sp.dma_start(g_src, src.rearrange("(p j) -> p j", p=P)).then_inc(S["g_in"], 16)
                sp.dma_start(g_dst, dst.rearrange("(p j) -> p j", p=P)).then_inc(S["g_in"], 16)
                sp.dma_start(g_w, edge_weight.rearrange("(p j) -> p j", p=P)).then_inc(S["g_in"], 16)
                for c in range(J // CJ):
                    if c >= 2:
                        sp.wait_ge(S["g_ea_used"], c - 1)
                    sp.dma_start(ea[:, c % 2], ea_v[:, c * CJ * D:(c + 1) * CJ * D]).then_inc(S[f"g_ea_in{c % 2}"], 16)
                for n in range(K0):
                    sp.wait_ge(S["table_ready"], n + 1)
                    sp.dma_start(g_table.rearrange("(t p) f -> p t f", p=P), h[:, :, :]).then_inc(S["table_in"], 16)
            with sp.If(way < 1):
                sp.wait_ge(S["rows_out"], 96)
                sp.wait_ge(S["l0_done"], 1)
                load_rows("l1", (1, 2))
            with sp.Else():
                sp.wait_ge(S["table_ready"], K0 + 1)
                sp.dma_start(kv_table.rearrange("(t p) f -> p t f", p=P), kvs[:, :, D:]).then_inc(S["table_in"], 16)
                sp.dma_start(g_table.rearrange("(t p) f -> p t f", p=P), kvs[:, :, 0:D]).then_inc(S["table_in"], 16)
            with sp.If(way < 1):
                sp.wait_ge(S["w_placed"], 1)
                sp.dma_start(wsl, w_table.rearrange("(r q) c -> r q c", r=L)).then_inc(S["wsl_in"], 16)
                load_rows("l2", (0,))
            with sp.Else():
                sp.wait_ge(S["table_ready"], K0 + 2)
                sp.dma_start(g_table.rearrange("(t p) f -> p t f", p=P), h[:, :, :]).then_inc(S["table_in"], 16)
            with sp.If(way < 1):
                load_rows("l3", (0,))
            with sp.Else():
                sp.wait_ge(S["table_ready"], K0 + 3)
                sp.dma_start(g_table.rearrange("(t p) f -> p t f", p=P), h[:, :, :]).then_inc(S["table_in"], 16)
            sp.wait_ge(S["out_ready"], 1)
            sp.dma_start(out.rearrange("(t p) f -> p t f", p=P), xs[:, :, :]).then_inc(S["out_in"], 16)
            sp.wait_ge(S["out_in"], 16)

        @block.gpsimd
        def _(pool):
            pool.iota(iota_i, pattern=[[1, Q]], base=0, channel_multiplier=0).then_inc(S["pool_step"], 1)
            pool.iota(lane_i[:, :], pattern=[[0, 1]], base=0, channel_multiplier=1).then_inc(S["pool_step"], 1)
            pool.iota(edge_i, pattern=[[1, J]], base=0, channel_multiplier=J).then_inc(S["pool_step"], 1)
            pool.memset(ones[:, :], 1.0).then_inc(S["pool_step"], 1)
            pool.memset(ones_b[:, :], 1.0).then_inc(S["pool_step"], 1)
            pool.memset(zero_c, 0.0).then_inc(S["pool_step"], 1)
            pool.memset(earlier, 1.0).then_inc(S["pool_step"], 1)
            pool.memset(ident[:, :], 0.0).then_inc(S["pool_step"], 1)
            pool.memset(pair[:, :], 0.0).then_inc(S["pool_step"], 1)
            pool.wait_ge(S["pool_step"], 9)
            pool.affine_select(out=ident[:, :], in_=ident[:, :], compare_op=ALU.not_equal, fill=1.0,
                               base=0, pattern=[[-1, L]], channel_multiplier=1).then_inc(S["pool_step"], 1)
            pool.affine_select(out=earlier, in_=earlier, compare_op=ALU.is_ge, fill=0.0,
                               base=-1, pattern=[[1, P]], channel_multiplier=-1).then_inc(S["pool_step"], 1)
            pool.affine_select(out=pair[:, :], in_=pair[:, :], compare_op=ALU.not_equal, fill=1.0,
                               base=0, pattern=[[-1, D]], channel_multiplier=1).then_inc(S["pool_step"], 1)
            pool.wait_ge(S["pool_step"], 12)
            pool.affine_select(out=pair[:, :], in_=pair[:, :], compare_op=ALU.not_equal, fill=1.0,
                               base=-D, pattern=[[-1, D]], channel_multiplier=1).then_inc(S["pool_step"], 1)
            pool.memset(blank, 0.0).then_inc(S["blank_ready"], 1)
            halves = 0
            pool.wait_ge(S["par_in"], 160)
            for c in range(J // CJ):
                chunk = ea_in[:, c % 2]
                pool.wait_ge(S[f"ea_in{c % 2}"], 16 * (c // 2 + 1))
                pool.tensor_tensor(chunk, chunk, psw[:, :].unsqueeze(1).to_broadcast([P, CJ, D]), ALU.mult).then_inc(S["ea_mult"], 1)
                pool.wait_ge(S["ea_mult"], c + 1)
                w = D // 2
                while w > 1:
                    pool.tensor_tensor(chunk[:, :, 0:w], chunk[:, :, 0:w], chunk[:, :, w:2 * w], ALU.add).then_inc(S["ea_half"], 1)
                    halves += 1
                    pool.wait_ge(S["ea_half"], halves)
                    w //= 2
                pool.tensor_tensor(wpa[:, c * CJ:(c + 1) * CJ, 1], chunk[:, :, 0], chunk[:, :, 1], ALU.add).then_inc(S["ea_used"], 1)
            way = path(pool)

            def gathers(n, p):
                k = 2 if p == "l1" else 1
                pool.wait_ge(S["table_in"], 16 * (n if p == "l0" else n + 1))
                with pool.Fori(0, J) as j:
                    pool.wait_ge(S["idx_ready"], n * J + 1 + j)
                    pool.sem_inc(S["gather_turn"], 1)
                    if p == "l1":
                        pool.indirect_dma_start(rows, None, kv_table, bass.IndirectOffsetOnAxis(idx_s, 0)).then_inc(S[f"gathered{n}"], 16)
                        pool.indirect_dma_start(rows_q, None, g_table, bass.IndirectOffsetOnAxis(idx_d, 0)).then_inc(S[f"gathered{n}"], 16)
                    else:
                        pool.indirect_dma_start(rows[:, 0:D], None, g_table, bass.IndirectOffsetOnAxis(idx_s, 0)).then_inc(S[f"gathered{n}"], 16)

            with pool.If(way < 1):
                pool.wait_ge(S["pa_ready"], 1)
                pool.wait_ge(S["w_cleared"], 16)

                def place_weights(g, half, used):
                    if used is not None:
                        pool.wait_ge(S[f"w_out{half}"], used * (16 * SU))
                        pool.sem_inc(S["place_turn"], 1)
                    at = 0 if used is None else used
                    pool.tensor_copy(s_idx[:, half], slot_i[:, bass.ds(g * SU, SU)]).then_inc(S[f"w_copied{half}"], 1)
                    pool.tensor_copy(s_val[:, half], wpa[:, bass.ds(g * SU, SU), :]).then_inc(S[f"w_copied{half}"], 1)
                    pool.wait_ge(S[f"w_copied{half}"], at * 2 + 2)
                    pool.sem_inc(S["place_turn"], 1)
                    for u in range(SU):
                        pool.indirect_dma_start(w_table, bass.IndirectOffsetOnAxis(s_idx[:, half, u:u + 1], 0), s_val[:, half, u], None
                                                ).then_inc(S[f"w_out{half}"], 16)
                place_weights(0, 0, None)
                place_weights(1, 1, None)
                place_weights(2, 0, 1)
                with pool.Fori(0, (J // SU - 3) // 2) as i:
                    place_weights(i * 2 + 3, 1, i + 1)
                    place_weights(i * 2 + 4, 0, i + 2)
                pool.wait_ge(S["w_out0"], 16 * SU * (J // SU // 2 + 1))
                pool.wait_ge(S["w_out1"], 16 * SU * (J // SU // 2))
                pool.sem_inc(S["w_placed"], 1)

                def layer1(s, par, on):
                    if 3 in on:
                        pool.wait_ge(S["l1_mid"], s - 2)
                        m, o = G1m[1 - par], msg1[:, 1 - par]
                        pool.tensor_tensor(o[:, :, 2 * M1:], m, o[:, :, M1:2 * M1], ALU.subtract).then_inc(S["l1_low"], 1)
                    if 2 in on:
                        pool.wait_ge(S["l1_high"], s - 1)
                        m, o = G1m[par], msg1[:, par]
                        pool.tensor_tensor(m, m, o[:, :, 0:M1], ALU.subtract).then_inc(S["l1_left"], 1)
                pool.sem_inc(S["l1_low"], 2)
                tile_steps(pool, layer1)

                for p in ("l2", "l3"):
                    def layer23(s, par, on):
                        if 2 in on:
                            pool.wait_ge(S[p + "_high"], s - 1)
                            pool.tensor_tensor(msg2[:, par, :, D:], msgf[:, par], msg2[:, par, :, 0:D], ALU.subtract
                                               ).then_inc(S[p + "_low"], 1)
                    pool.sem_inc(S[p + "_low"], 2)
                    tile_steps(pool, layer23)
            with pool.Else():
                pool.wait_ge(S["g_src_free"], 1)
                pool.iota(node_i, pattern=[[1, N]], base=0, channel_multiplier=0).then_inc(S["g_pool"], 1)
                pool.memset(zeros, 0.0).then_inc(S["g_pool"], 1)
                for n in range(K0):
                    gathers(n + 1, "l0")
                gathers(K0 + 1, "l1")
                gathers(K0 + 2, "l2")
                gathers(K0 + 3, "l3")

        @block.scalar
        def _(act):
            def std_of_var(n):
                act.wait_ge(S["var_ready"], n)
                act.activation(std[:, :], var[:, :], ACT.Sqrt).then_inc(S["std_ready"], 1)

            def edge_layer(p):
                groups = GROUPS[p]
                ng = len(groups)
                m1 = 3 * M1 if p == "l1" else 2 * D
                if p == "l1":
                    act.sem_inc(S["l1_rows"], ng)
                else:
                    act.sem_inc(S[p + "_last_rows"], 1)
                act.sem_inc(S[p + "_sums"], 2)

                def body(s, par, on):
                    def rows(a, b):
                        for m in range(a, b):
                            act.wait_ge(S["l1_gath"], (s - 1) * ng + (2 * ng + m + 1))
                            if m == 0:
                                act.wait_ge(S["l1_val"], s)
                            act.activation(G1[:, 1 - par, 2 * m:2 * m + 2, :],
                                           ps[:, m % RING, 0:2 * 3 * D].rearrange("p (c f) -> p c f", c=2),
                                           ACT.Copy).then_inc(S["l1_rows"], 1)
                    if p == "l1":
                        if 1 in on:
                            rows(0, RING)
                        if 3 in on:
                            act.wait_ge(S["l1_left"], s - 2)
                            act.activation(msg1[:, 1 - par, :, M1:2 * M1], G1m[1 - par], ACT.Copy).then_inc(S["l1_mid"], 1)
                        if 2 in on:
                            act.wait_ge(S["l1_logit"], s - 1)
                            act.wait_ge(S["l1_low"], s - 1)
                            act.activation(G1m[par][:, :, D:M1], logit, ACT.Exp).then_inc(S["l1_exp"], 1)
                        if 1 in on:
                            rows(RING, ng)
                        if 2 in on:
                            act.wait_ge(S["l1_val"], s + 1)
                            act.wait_ge(S["l1_scat"], s - 1)
                            act.activation(msg1[:, par, :, 0:M1], G1m[par], ACT.Copy).then_inc(S["l1_high"], 1)
                    elif 2 in on:
                        act.wait_ge(S[p + "_low"], s - 1)
                        act.wait_ge(S[p + "_gath"], (s - 2) * ng + 3 * ng)
                        for k in range(groups[-1]):
                            c = C - groups[-1] + k
                            last = act.activation(msgf[:, par, c, :], ps[:, ng - 1, k * D:(k + 1) * D], ACT.Copy,
                                                  scale=wsl[:, bass.ds((s - 2) * C + c, 1), 0 if p == "l2" else 1])
                        last.then_inc(S[p + "_last_rows"], 1)
                        act.wait_ge(S[p + "_last_rows"], s)
                        act.wait_ge(S[p + "_rows"], (s - 1) * (ng - 1) + (ng - 1))
                        act.wait_ge(S[p + "_scat"], s - 1)
                        act.activation(msg2[:, par, :, 0:D], msgf[:, par], ACT.Copy).then_inc(S[p + "_high"], 1)
                    if 4 in on:
                        act.wait_ge(S[p + "_scat"], s - 1)
                        act.activation(sums[:, bass.ds(s - 4, 1), 0:m1], ps[0:P, RING + par, 0:m1].unsqueeze(1),
                                       ACT.Copy).then_inc(S[p + "_sums"], 1)
                tile_steps(act, body)

            way = path(act)
            with act.If(way < 1):
                act.dma_start(edge_place.rearrange("(p j) c -> p (j c)", p=P), place.rearrange("p j c -> p (j c)")
                              ).then_inc(S["place_out"], 16)
                act.activation(rep_s, iota_h[0:P, 0:L].unsqueeze(2).to_broadcast([P, L, JP]), ACT.Copy).then_inc(S["rep_ready"], 1)
                act.wait_ge(S["place_out"], 16)
                act.dma_start(placed, edge_place.rearrange("(b r p) c -> r b (p c)", r=BT * JT, p=P)).then_inc(S["place_back"], 16)
            std_of_var(1)
            with act.If(way < 1):
                act.wait_ge(S["ln0_done"], 1)
                act.activation(adj_rep, iota_h[:, 0:P].unsqueeze(2).to_broadcast([L, P, C]), ACT.Copy).then_inc(S["rep_ready"], 1)
                for e in range(3):
                    for hlf in range(2):
                        act.wait_ge(S["rowT_ps"], 2 * e + hlf + 1)
                        n = min(4, QT - 4 * hlf)
                        for c in range(4 * hlf, 4 * hlf + n):
                            k = min(L, Q - c * L)
                            last = act.activation(rowT[0:k, e, c, :], ps[0:k, 2 + 2 * e + hlf, (c % 4) * L:(c % 4 + 1) * L], ACT.Copy)
                        last.then_inc(S["rowT_ready"], 1)
                act.wait_ge(S["ea_used"], J // CJ)
                act.activation(wpa[:, :, 1], wpa[:, :, 1], ACT.Sigmoid).then_inc(S["pa_ready"], 1)
                act.sem_inc(S["adj_taken"], 6)
                with act.Fori(0, T) as d:
                    for g in range(6):
                        act.wait_ge(S["adj_mm"], d * 7 + (g + 8))
                        act.activation(adj[:, 4 * g:4 * g + 4, bass.ds(d * P, P)],
                                       ps[0:P, g, 0:4 * P].rearrange("p (s d) -> p s d", s=4), ACT.Copy).then_inc(S["adj_taken"], 1)
            std_of_var(2)
            with act.If(way < 1):
                act.wait_ge(S["g_ready"], 1)
                act.activation(base, h, ACT.Copy, scale=ALPHA).then_inc(S["base_ready"], 1)
                act.sem_inc(S["mains_taken"], NCH)

                def chunks(i):
                    for u in range(2):
                        for c in range(NCH):
                            n = u * NCH + c
                            act.wait_ge(S["mains"], i * (2 * NCH) + (n + 1))
                            act.wait_ge(S["combined"], i * (2 * NCH) + (n + 1))
                            w = min(CH, T - CH * c) * P
                            act.activation(part[:, n % 2, 0:w], ps[:, c, 0:w], ACT.Copy).then_inc(S["mains_taken"], 1)
                act.wait_ge(S["rows_out"], 96)
                with act.Fori(0, K0 // 2) as i:
                    chunks(i)
            with act.Else():
                act.wait_ge(S["g_z_ready"], 1)
                act.activation(g_pa, g_z, ACT.Sigmoid).then_inc(S["g_pa_ready"], 1)
            with act.If(way < 1):
                act.wait_ge(S["l0_done"], 1)
                act.activation(rep_i, iota_h[:, 0:P].unsqueeze(2).to_broadcast([L, P, C]), ACT.Copy).then_inc(S["rep_ready"], 1)
            std_of_var(3)
            take(act, "a", "l1_h", lambda t, n, b: act.activation(
                hT[:, t:t + n, :], ps[0:D, b, 0:n * P].rearrange("p (t n) -> p t n", t=n), ACT.Copy))
            take(act, "a", "l1_qkv", lambda t, n, b: act.activation(
                kvs[:, t:t + n, :], ps[0:P, b, 0:n * 3 * D].rearrange("p (t n) -> p t n", t=n), ACT.Copy))
            with act.If(way < 1):
                for i in range(3):
                    act.wait_ge(S["scaled"], 1)
                    act.activation(parts[:, :, 0, i * D:(i + 1) * D], kvs[:, :, i * D:(i + 1) * D], ACT.Copy,
                                   scale=top_r[0:P, i:i + 1]).then_inc(S["high_ready"], 1)
                edge_layer("l1")
            with act.Else():
                with act.Fori(0, J) as j:
                    act.wait_ge(S["logit_ready"], j + 1)
                    act.activation(msg[:, D:M1], att2, ACT.Exp).then_inc(S["expd"], 1)
            std_of_var(4)
            with act.If(way < 1):
                act.wait_ge(S["scaled"], 2)
                act.activation(parts[:, :, 0, 0:D], h, ACT.Copy, scale=GSCALE).then_inc(S["high_ready"], 1)
                edge_layer("l2")
            act.wait_ge(S["l2_done"], 1)
            act.activation(cat[:, :, 0:D], h, ACT.Copy).then_inc(S["cat_norm"], 1)
            take(act, "a", "l2_cat", lambda t, n, b: act.activation(
                catT[:, t:t + n, :], ps[:, b, 0:n * P].rearrange("p (t n) -> p t n", t=n), ACT.Copy))
            std_of_var(5)
            with act.If(way < 1):
                act.wait_ge(S["scaled"], 3)
                act.activation(parts[:, :, 0, 0:D], h, ACT.Copy, scale=top_r[0:P, 0:1]).then_inc(S["high_ready"], 1)
                edge_layer("l3")

        @block.vector
        def _(vec):
            steps = [0]

            def step(ins):
                steps[0] += 1
                ins.then_inc(S["vec_step"], 1)
                vec.wait_ge(S["vec_step"], steps[0])

            class Chain:
                def __init__(self, name):
                    self.name, self.n = name, 0

                def __call__(self, ins, at=None):
                    self.n += 1
                    ins.then_inc(S[self.name], 1)
                    vec.wait_ge(S[self.name], self.n if at is None else at + self.n)

            def per_node(v):
                return v[:, :].unsqueeze(2).to_broadcast([P, T, D])

            n_norms = [0]

            def std_from_act():
                n_norms[0] += 1
                vec.wait_ge(S["std_ready"], n_norms[0])

            def layer_norm(weight=None):
                step(vec.tensor_reduce(mean[:, :], xs[:, :, :], AX.X, ALU.add))
                step(vec.tensor_scalar(mean[:, :], mean[:, :], 1.0 / D, None, ALU.mult))
                step(vec.tensor_tensor(h[:, :, :], xs[:, :, :], per_node(mean), ALU.subtract))
                step(vec.tensor_tensor(base[:, :, :], h[:, :, :], h[:, :, :], ALU.mult))
                step(vec.tensor_reduce(var[:, :], base[:, :, :], AX.X, ALU.add))
                vec.tensor_scalar(var[:, :], var[:, :], 1.0 / D, EPS, ALU.mult, ALU.add).then_inc(S["var_ready"], 1)
                std_from_act()
                step(vec.reciprocal(rstd[:, :], std[:, :]))
                if weight is not None:
                    step(vec.tensor_tensor(rstd[:, :], rstd[:, :], weight[:, :], ALU.mult))
                step(vec.scalar_tensor_tensor(h[:, :, :], h[:, :, :], 0.0, per_node(rstd), ALU.max, ALU.mult))

            taken, chained = [0], [0]

            def gather_aggregate(p):
                n = taken[0]
                b = n * J
                k = 32 if p == "l1" else 16
                with vec.Fori(0, J) as j:
                    vec.wait_ge(S["scattered"], b + j + 1)
                    here, there, here_f = (g_src, g_dst, g_srcf) if p == "l1" else (g_dst, g_src, g_dstf)
                    vec.tensor_copy(idx_d, here[:, bass.ds(j, 1)])
                    vec.tensor_copy(idx_s, there[:, bass.ds(j, 1)]).then_inc(S["idx_ready"], 1)
                    vec.tensor_scalar(hit, node_f, here_f[:, bass.ds(j, 1)], None, ALU.is_equal).then_inc(S["hit_ready"], 1)
                    if p == "deg":
                        vec.memset(msg[:, 0:1], 1.0).then_inc(S["msg_ready"], 1)
                    else:
                        vec.wait_ge(S[f"gathered{n}"], k + j * k)
                    if p == "l0":
                        vec.tensor_copy(msg[:, 0:D], rows[:, 0:D]).then_inc(S["msg_ready"], 1)
                    if p == "l2":
                        vec.tensor_scalar(msg[:, 0:D], rows[:, 0:D], g_w[:, bass.ds(j, 1)], None, ALU.mult).then_inc(S["msg_ready"], 1)
                    if p == "l3":
                        vec.tensor_scalar(msg[:, 0:D], rows[:, 0:D], g_pa[:, bass.ds(j, 1)], None, ALU.mult).then_inc(S["msg_ready"], 1)
                    if p == "l1":
                        vec.tensor_tensor(qk, rows[:, 0:D], rows_q, ALU.mult).then_inc(S["qk_step"], 1)
                        vec.wait_ge(S["qk_step"], j * 2 + 1)
                        vec.tensor_reduce(att, qk.rearrange("p (a d) -> p a d", a=HEADS), AX.X, ALU.add).then_inc(S["qk_step"], 1)
                        vec.wait_ge(S["qk_step"], j * 2 + 2)
                        vec.tensor_scalar(att2, att, -10.0, 10.0, ALU.max, ALU.min).then_inc(S["logit_ready"], 1)
                        vec.wait_ge(S["expd"], j + 1)
                        vec.tensor_tensor(msg[:, 0:D].rearrange("p (a d) -> p a d", a=HEADS),
                                          rows[:, D:].rearrange("p (a d) -> p a d", a=HEADS),
                                          msg[:, D:M1].unsqueeze(2).to_broadcast([P, HEADS, HD]), ALU.mult).then_inc(S["msg_ready"], 1)
                taken[0] += 1
                vec.wait_ge(S["scattered"], taken[0] * J + 1)
                for q in range(NBANK):
                    last = vec.tensor_copy(agg[:, q * TB:(q + 1) * TB, :],
                                           acc[0:P, q, 0:TB * M1].rearrange("p (t f) -> p t f", t=TB))
                last.then_inc(S["acc_taken"], 1)
                vec.wait_ge(S["acc_taken"], taken[0])

            def low_part(done, x_ap, scale, a, chain):
                vec.wait_ge(S["high_ready"], done)
                chain(vec.scalar_tensor_tensor(parts[:, :, 1, a:a + D], x_ap, scale, parts[:, :, 0, a:a + D], ALU.mult, ALU.subtract))

            tops = [0]

            def spread_top(n, k, dest, chain):
                tops[0] += 1
                vec.sem_inc(S["top_go"], 1)
                vec.wait_ge(S["top_T"], tops[0])
                chain(vec.tensor_reduce(top_g[0:k, 3:4], ps[0:k, 0, 0:n], AX.X, ALU.max))
                chain(vec.tensor_scalar(top_g[0:k, 3:4], top_g[0:k, 3:4], 1e-30, None, ALU.max))
                vec.tensor_scalar(top_g[0:k, 0:k], ident[0:k, 0:k], top_g[0:k, 3:4], None, ALU.mult).then_inc(S["top_d"], 1)
                vec.wait_ge(S["top_all"], tops[0])
                chain(vec.tensor_copy(dest, ps[:, 1, 0:k]))

            def edge_layer(p, chain):
                ng = len(GROUPS[p])
                ends = 2 if p == "l1" else 1
                lanes = sls_h if p == "l1" else dl_h
                if p == "l1":
                    vec.sem_inc(S["l1_val"], 2)
                else:
                    vec.sem_inc(S[p + "_rows"], ng - 1)

                def ohT_of(s, par, e):
                    if e == 0:
                        vec.wait_ge(S[p + "_gath"], s * ng + ng)
                    if p == "l1":
                        vec.wait_ge(S[f"l1_row{e}"], s * 16 + 16)
                    else:
                        vec.wait_ge(S[p + f"_row{par}"], s * 8 + (16 - 8 * par))
                    done = vec.tensor_scalar(ohT[:, par, e], rowbc[:, e if p == "l1" else par], lane[0:P, :], None, ALU.is_equal)
                    done.then_inc(S[p + "_ohT" if e == ends - 1 else "l1_first"], 1)

                def ohd_of(s, par):
                    vec.wait_ge(S[p + "_scat"], s - 1)
                    vec.tensor_tensor(ohd[:, par], rep_i, lanes[:, bass.ds((s - 2) * C, C)].unsqueeze(1).to_broadcast([L, P, C]),
                                      ALU.is_equal).then_inc(S[p + "_ohd"], 1)

                def layer1(s, par, on):
                    if 2 in on:
                        vec.wait_ge(S["l1_rows"], (s - 1) * ng + ng)
                        vec.tensor_tensor(prod, G1[:, par, :, 0:D], G1[:, par, :, 2 * D:], ALU.mult).then_inc(S["l1_step"], 1)
                    if 0 in on:
                        ohT_of(s, par, 0)
                    if 2 in on:
                        vec.wait_ge(S["l1_step"], (s - 2) * 3 + 1)
                        vec.tensor_reduce(logit.rearrange("p c a -> p (c a)"),
                                          prod.rearrange("p c (a d) -> p (c a) d", a=HEADS), AX.X, ALU.add).then_inc(S["l1_step"], 1)
                    if 0 in on:
                        ohT_of(s, par, 1)
                    if 2 in on:
                        vec.wait_ge(S["l1_step"], (s - 2) * 3 + 2)
                        vec.tensor_scalar(logit, logit, top_r[:, 0:1], -10.0, ALU.mult, ALU.max).then_inc(S["l1_step"], 1)
                        vec.wait_ge(S["l1_step"], (s - 2) * 3 + 3)
                        vec.tensor_scalar(logit, logit, 10.0, None, ALU.min).then_inc(S["l1_logit"], 1)
                        vec.wait_ge(S["l1_exp"], s - 1)
                        vec.tensor_tensor(G1m[par][:, :, 0:D].rearrange("p c (a d) -> p c a d", a=HEADS),
                                          G1[:, par, :, D:2 * D].rearrange("p c (a d) -> p c a d", a=HEADS),
                                          G1m[par][:, :, D:M1].unsqueeze(3).to_broadcast([L, C, HEADS, HD]), ALU.mult
                                          ).then_inc(S["l1_val"], 1)
                        ohd_of(s, par)

                def layer23(s, par, on):
                    if 2 in on:
                        vec.wait_ge(S[p + "_low"], s - 1)
                        c = 0
                        for m, n in enumerate(GROUPS[p][:-1]):
                            vec.wait_ge(S[p + "_gath"], (s - 2) * ng + (2 * ng + m + 1))
                            w = wsl[:, bass.ds((s - 2) * C + c, n), 0 if p == "l2" else 1]
                            vec.tensor_tensor(msgf[:, par, c:c + n, :], ps[:, m, 0:n * D].rearrange("p (c f) -> p c f", c=n),
                                              w.unsqueeze(2).to_broadcast([L, n, D]), ALU.mult).then_inc(S[p + "_rows"], 1)
                            c += n
                    if 0 in on:
                        ohT_of(s, par, 0)
                    if 2 in on:
                        ohd_of(s, par)
                tile_steps(vec, layer1 if p == "l1" else layer23)
                vec.wait_ge(S[p + "_sums"], T + 2)
                if p == "l1":
                    chain(vec.tensor_tensor(agg[:, 0:T, :], sums[:, :, M1:2 * M1], sums[:, :, 2 * M1:], ALU.add))
                    chain(vec.tensor_tensor(agg[:, 0:T, :], agg[:, 0:T, :], sums[:, :, 0:M1], ALU.add))
                else:
                    chain(vec.tensor_tensor(agg[:, 0:T, 0:D], sums[:, :, 0:D], sums[:, :, D:2 * D], ALU.add))

            vec.wait_ge(S["idx_in"], 32)
            vec.tensor_copy(src_f, src_i)
            step(vec.tensor_copy(dst_f, dst_i))
            for f, tile, ln in ((src_f, st, s_l), (dst_f, dt_, d_l)):
                step(vec.tensor_scalar(tile, f, -float(P // 2), 1.0 / P, ALU.add, ALU.mult))
                step(vec.tensor_scalar(tile, tile, ROUND, -ROUND, ALU.add, ALU.add))
                step(vec.scalar_tensor_tensor(ln, tile, -float(P), f, ALU.mult, ALU.add))
            vec.memset(same[:, 0:1], 1.0)
            vec.tensor_tensor(same[:, 1:J], dt_[:, 1:J], dt_[:, 0:J - 1], ALU.is_equal)
            step(vec.tensor_scalar(last_run, dt_, dt_[:, J - 1:J], None, ALU.is_equal))
            for s in range(T):
                last = vec.tensor_scalar(hits[:, s, :], st, float(s), None, ALU.is_equal)
            step(last)
            step(vec.tensor_tensor(picked, hits, last_run.unsqueeze(1).to_broadcast([P, T, J]), ALU.mult))
            n = J - 1
            while n % 2 == 0:
                n //= 2
                step(vec.tensor_tensor(picked[:, :, 0:n], picked[:, :, 0:n], picked[:, :, n:2 * n], ALU.add))
            step(vec.tensor_reduce(run_end, picked[:, :, 0:n], AX.X, ALU.add))
            vec.tensor_tensor(run_end, run_end, picked[:, :, J - 1], ALU.add)
            vec.wait_ge(S["pool_step"], 13)
            vec.tensor_scalar(first_d, ident[0:P, 0:P], dt_[:, 0:1], None, ALU.mult).then_inc(S["first_d"], 1)
            vec.wait_ge(S["first_ps"], 1)
            step(vec.tensor_scalar(first_r, ps[0:P, 0, 0:P], dt_[:, J - 1:J], None, ALU.is_lt))
            step(vec.tensor_tensor(first_r, first_r, earlier, ALU.mult))
            vec.tensor_reduce(bad[:, 0:1], first_r, AX.X, ALU.add)
            step(vec.tensor_scalar(link_m, ps[0:P, 0, 0:P], dt_[:, J - 1:J], None, ALU.is_equal))
            vec.tensor_tensor(link_m, link_m, earlier, ALU.mult).then_inc(S["link_ready"], 1)
            vec.wait_ge(S["carry_ps"], 1)
            step(vec.tensor_copy(carry, ps[0:P, 1, 0:T]))
            for s in range(T):
                last = vec.tensor_tensor_scan(runs[:, s, :], same, hits[:, s, :], carry[:, s:s + 1], ALU.mult, ALU.add)
            step(last)
            step(vec.tensor_tensor(picked, hits, runs, ALU.mult))
            n = T // 2
            while n >= 3:
                step(vec.tensor_tensor(picked[:, 0:n, :], picked[:, 0:n, :], picked[:, n:2 * n, :], ALU.add))
                n //= 2
            for s in (1, 2):
                step(vec.tensor_tensor(picked[:, 0, :], picked[:, 0, :], picked[:, s, :], ALU.add))
            step(vec.scalar_tensor_tensor(rank, picked[:, 0, :], -1.0, picked[:, T - 1, :], ALU.add, ALU.add))
            vec.tensor_scalar(over, rank, float(L), None, ALU.is_ge)
            step(vec.tensor_tensor(tmp_j, dt_, st, ALU.not_equal))
            step(vec.tensor_tensor(tmp_j, tmp_j, over, ALU.mult))
            step(vec.tensor_reduce(bad[:, 1:2], tmp_j, AX.X, ALU.add))
            step(vec.tensor_scalar(tmp_j, rank, 2.0 * L, None, ALU.is_ge))
            step(vec.tensor_reduce(bad[:, 2:3], tmp_j, AX.X, ALU.add))
            step(vec.tensor_tensor(tmp_j[:, 1:J], dt_[:, 1:J], dt_[:, 0:J - 1], ALU.is_lt))
            step(vec.tensor_reduce(bad[:, 3:4], tmp_j[:, 1:J], AX.X, ALU.add))
            step(vec.tensor_copy(first_t, edge_i))
            step(vec.tensor_scalar(first_t, first_t, -float(JH * P + P * JT // 2), 1.0 / (P * JT), ALU.add, ALU.mult))
            step(vec.tensor_scalar(first_t, first_t, ROUND, -ROUND, ALU.add, ALU.add))
            step(vec.tensor_scalar(first_t, first_t, 0.0, float(T - 2), ALU.max, ALU.min))
            step(vec.tensor_tensor(tmp_j, dt_, first_t, ALU.subtract))
            step(vec.scalar_tensor_tensor(tmp_j, tmp_j, -1.0, tmp_j, ALU.add, ALU.mult))
            step(vec.tensor_reduce(bad[:, 4:5], tmp_j, AX.X, ALU.add))
            vec.tensor_reduce(run_end[:, 0:1], bad, AX.X, ALU.add).then_inc(S["bad_ready"], 1)
            vec.wait_ge(S["bad_ps"], 1)
            step(vec.tensor_scalar(flag[:, :], ps[0:1, 2, 0:1], 1.0, None, ALU.min))
            step(vec.tensor_scalar(tmp_j, st, -1.0, float(T), ALU.mult, ALU.add))
            step(vec.tensor_tensor(tmp_j, tmp_j, over, ALU.mult))
            step(vec.tensor_tensor(tmp_j, tmp_j, st, ALU.add))
            vec.scalar_tensor_tensor(place[:, :, 1], dt_, float(C), tmp_j, ALU.mult, ALU.add)
            step(vec.scalar_tensor_tensor(place[:, :, 0], over, -float(L), rank, ALU.mult, ALU.add))
            step(vec.scalar_tensor_tensor(tmp_j, place[:, :, 0], float(Q), place[:, :, 1], ALU.mult, ALU.add))
            step(vec.tensor_copy(slot_i[:, :], tmp_j))
            vec.scalar_tensor_tensor(place[:, :, 1], first_t, -float(C), place[:, :, 1], ALU.mult, ALU.add)
            step(vec.scalar_tensor_tensor(place[:, :, 2], s_l, 128.0, d_l, ALU.mult, ALU.add))
            vec.wait_ge(S["edge_in"], 16)
            vec.tensor_copy(wpa[:, :, 0], edge_w)
            vec.tensor_copy(lane[:, :], lane_i[:, :])
            step(vec.tensor_copy(iota_h[:, :], iota_i))
            vec.wait_ge(S["w_cleared"], 16)
            vec.sem_inc(S["flag_ready"], 1)
            way = path(vec)

            vec.wait_ge(S["x_in"], 16)
            vec.wait_ge(S["par_in"], 160)
            layer_norm()
            vec.sem_inc(S["ln0_done"], 1)

            with vec.If(way < 1):
                fast = Chain("fast_step")
                vec.memset(lane_c[:, :, JT:JP], 0.0)
                vec.memset(col_c[:, :, JT:JP], 0.0)
                vec.memset(load_c[:, :, JT:JP], 0.0)
                vec.wait_ge(S["place_T"], 3)

                def column(c):
                    return ps[0:P, c, 0:J].rearrange("p (t k) -> p t k", k=JT)
                vec.tensor_copy(lane_c[:, :, 0:JT], column(0))
                vec.tensor_scalar(load_i, ps[0:P, 2, 0:J], 128.0, 65536.0, ALU.add, ALU.mult)
                fast(vec.tensor_copy(col_c[:, :, 0:JT], column(1)))
                fast(vec.tensor_copy(load_c[:, :, 0:JT], load_i.bitcast(F32).rearrange("p (t k) -> p t k", k=JT)))
                vec.wait_ge(S["rep_ready"], 1)

                def sort_tile(t, par):
                    def over(tab, n):
                        return tab[:, bass.ds(t, 1), :].to_broadcast([P, n, JP])
                    vec.wait_ge(S["to_slot"], t + 1)
                    vec.tensor_tensor(hit_col, rep_s[:, 0:W2, :], over(col_c, W2), ALU.is_equal).then_inc(S["hit_col"], 1)
                    vec.wait_ge(S["sorted"], t + 1)
                    vec.tensor_tensor(to_lane[:, par], rep_s, over(lane_c, L), ALU.is_equal).then_inc(S["to_lane"], 1)
                    vec.wait_ge(S["hit_col"], t + 1)
                    vec.tensor_tensor(to_col[:, par], hit_col, over(load_c, W2), ALU.mult).then_inc(S["to_slot"], 1)
                vec.sem_inc(S["to_slot"], 1)
                with vec.Fori(0, T // 2) as i:
                    for u in range(2):
                        sort_tile(i * 2 + u, u)
                sort_tile(T - 1, (T - 1) % 2)
                vec.wait_ge(S["sorted"], T + 2)
                vec.tensor_copy(bits[:, 0:TA * C], ps[:, 3, 0:TA * C])
                fast(vec.tensor_copy(bits[:, TA * C:Q], ps[:, 4, C:(T - TA + 1) * C]))
                shared = bits[:, (TA - 1) * C:TA * C]
                fast(vec.tensor_tensor(shared, shared, ps[:, 4, 0:C], ALU.add))
                vec.tensor_scalar(bits_a, bits.bitcast(I32), 23, None, ALU.logical_shift_right)
                fast(vec.tensor_scalar(bits_b, bits.bitcast(I32), 16, 127, ALU.logical_shift_right, ALU.bitwise_and))
                vec.tensor_copy(sl, bits_a)
                fast(vec.tensor_copy(dl, bits_b))
                fast(vec.tensor_scalar(sl, sl, -1.0, None, ALU.add))
                fast(vec.tensor_scalar(bits, sl, -1.0, None, ALU.is_equal))
                fast(vec.tensor_tensor(dl, dl, bits, ALU.subtract))
                vec.tensor_copy(sl_h[:, :], sl)
                vec.tensor_copy(dl_h[:, :], dl)
                for tab, tab_s in ((sl, sl_s), (dl, dl_s)):
                    by_tile = tab[:, :].rearrange("p (d c) -> p c d", c=C)
                    vec.tensor_copy(tab_s[:, :, 0:T], by_tile[:, 0:T, :])
                    fast(vec.tensor_copy(tab_s[:, :, T], by_tile[:, T, :]))
                fast(vec.tensor_copy(sls_h[:, :].rearrange("p (s c) -> p s c", c=C), sl_s))
                vec.sem_inc(S["slots_ready"], 1)
                def one_hots(d, half):
                    c, n = sum(KG[:half]), KG[half]
                    for e, lanes in enumerate((sl_h, dl_h)):
                        vec.tensor_tensor(adj_oh[half][e], adj_rep[:, :, c:c + n],
                                          lanes[:, bass.ds(d * C + c, n)].unsqueeze(1).to_broadcast([L, P, n]),
                                          ALU.is_equal).then_inc(S["adj_oh"], 1)

                def finish(d, used):
                    vec.wait_ge(S["adj_mm"], used)
                    vec.tensor_copy(adj[:, T - 1, bass.ds(d * P, P)], ps[0:P, 6, 0:P]).then_inc(S["adj_last"], 1)
                    vec.tensor_copy(deg[:, bass.ds(d, 1)], ps[0:P, 7, 0:1])
                    vec.wait_ge(S["adj_last"], d + 1)
                    vec.wait_ge(S["adj_taken"], d * 6 + 12)
                    here = adj[:, bass.ds(d, 1), bass.ds(d * P, P)].rearrange("p s d -> p (s d)")
                    vec.tensor_tensor(here, here, ps[0:P, 6, P:2 * P], ALU.add).then_inc(S["adj_done"], 1)
                vec.wait_ge(S["rep_ready"], 2)
                vec.wait_ge(S["ea_used"], J // CJ)
                one_hots(0, 0)
                one_hots(0, 1)
                with vec.Fori(0, T - 1) as i:
                    vec.wait_ge(S["adj_used"], i + 1)
                    one_hots(i + 1, 0)
                    finish(i, i * 7 + 14)
                    one_hots(i + 1, 1)
                finish(T - 1, (T - 1) * 7 + 14)
                vec.wait_ge(S["adj_done"], T + 1)
                fast(vec.tensor_scalar(deg[:, :], deg[:, :], 1.0, None, ALU.max))
            with vec.Else():
                gen = Chain("gen_step")
                vec.sem_inc(S["g_src_free"], 1)
                vec.sem_inc(S["scattered"], 1)
                vec.wait_ge(S["g_in"], 48)
                vec.tensor_copy(g_dstf, g_dst)
                vec.tensor_copy(g_srcf, g_src)
                vec.wait_ge(S["g_pool"], 2)
                gen(vec.tensor_copy(node_f, node_i))
                for c in range(J // CJ):
                    vec.wait_ge(S[f"g_ea_in{c % 2}"], 16 * (c // 2 + 1))
                    ea_c = ea[:, c % 2].rearrange("p (j f) -> p j f", j=CJ)
                    gen(vec.tensor_tensor(ea_c, ea_c, psw[:, :].unsqueeze(1).to_broadcast([P, CJ, D]), ALU.mult))
                    vec.tensor_reduce(g_z[:, c * CJ:(c + 1) * CJ], ea_c, AX.X, ALU.add).then_inc(S["g_ea_used"], 1)
                vec.wait_ge(S["g_ea_used"], J // CJ)
                vec.sem_inc(S["g_z_ready"], 1)
                gather_aggregate("deg")
                gen(vec.tensor_scalar(deg[:, :], agg[:, 0:T, 0], 1.0, None, ALU.max))
            vec.tensor_copy(var[:, :], deg[:, :]).then_inc(S["var_ready"], 1)
            std_from_act()
            vec.reciprocal(rdeg[:, :], deg[:, :])
            step(vec.reciprocal(norm[:, :], std[:, :]))

            with vec.If(way < 1):
                fast(vec.tensor_scalar(coef[:, :], norm[:, :], GSCALE, None, ALU.mult))
                fast(vec.tensor_tensor(h[:, :, :], h[:, :, :], per_node(coef), ALU.mult))
                vec.sem_inc(S["g_ready"], 1)
                fast(vec.tensor_copy(hl[0:P, 0, :, 0:D], h[:, :, :]))
                fast(vec.tensor_tensor(hl[0:P, 0, :, D:], h[:, :, :], hl[0:P, 0, :, 0:D], ALU.subtract))
                fast(vec.tensor_scalar(coef[:, :], rdeg[:, :], 1 - ALPHA, None, ALU.mult))
                vec.sem_inc(S["hl_ready"], NCH)
                vec.sem_inc(S["sums_read"], 1)
                vec.wait_ge(S["base_ready"], 1)
                with vec.Fori(0, K0 // 2) as i:
                    for u in range(2):
                        for c in range(NCH):
                            n = u * NCH + c
                            k = min(CH, T - CH * c)
                            t = slice(CH * c, CH * c + k)
                            turned = ps[0:P, 7, 0:k * D].rearrange("p (t f) -> p t f", t=k)
                            vec.wait_ge(S["combined"], i * (2 * NCH) + (n + 3))
                            vec.tensor_tensor(h[:, t, :], turned, coef[:, t].unsqueeze(2).to_broadcast([P, k, D]), ALU.mult
                                              ).then_inc(S["sums_read"], 1)
                            vec.wait_ge(S["sums_read"], i * (2 * NCH) + (n + 2))
                            vec.tensor_tensor(h[:, t, :], h[:, t, :], base[:, t, :], ALU.add).then_inc(S["g_step"], 1)
                            vec.wait_ge(S["g_step"], i * (4 * NCH) + (2 * n + 1))
                            vec.tensor_copy(hl[0:P, 1 - u, t, 0:D], h[:, t, :]).then_inc(S["g_step"], 1)
                            vec.wait_ge(S["g_step"], i * (4 * NCH) + (2 * n + 2))
                            vec.tensor_tensor(hl[0:P, 1 - u, t, D:], h[:, t, :], hl[0:P, 1 - u, t, 0:D], ALU.subtract
                                              ).then_inc(S["hl_ready"], 1)
                vec.wait_ge(S["hl_ready"], (K0 + 1) * NCH)
                vec.sem_inc(S["l0_done"], 1)
                fast(vec.tensor_scalar(coef[:, :], std[:, :], 1.0 / GSCALE, None, ALU.mult))
                fast(vec.tensor_tensor(h[:, :, :], h[:, :, :], per_node(coef), ALU.mult))
            with vec.Else():
                vec.tensor_scalar(base[:, :, :], h[:, :, :], ALPHA, None, ALU.mult)
                gen(vec.tensor_scalar(coef[:, :], norm[:, :], 1 - ALPHA, None, ALU.mult))
                for it in range(K0):
                    vec.tensor_tensor(h[:, :, :], h[:, :, :], per_node(norm), ALU.mult).then_inc(S["table_ready"], 1)
                    gather_aggregate("l0")
                    gen(vec.tensor_tensor(h[:, :, :], agg[:, 0:T, 0:D], per_node(coef), ALU.mult))
                    gen(vec.tensor_tensor(h[:, :, :], h[:, :, :], base[:, :, :], ALU.add))
            step(vec.tensor_tensor(xs[:, :, :], xs[:, :, :], h[:, :, :], ALU.add))

            layer_norm()
            vec.sem_inc(S["h_ready"], 1)
            take(vec, "v", "l1_h", lambda t, n, b: vec.tensor_copy(
                hT[:, t:t + n, :], ps[0:D, b, 0:n * P].rearrange("p (t n) -> p t n", t=n)))
            take(vec, "v", "l1_qkv", lambda t, n, b: vec.tensor_copy(
                kvs[:, t:t + n, :], ps[0:P, b, 0:n * 3 * D].rearrange("p (t n) -> p t n", t=n)))
            all_taken(vec, "l1_qkv")
            with vec.If(way < 1):
                fast(vec.tensor_reduce(top_r[0:P, 0:3], kvs[:, :, :].rearrange("p t (i d) -> p i t d", i=3), AX.XY, ALU.max,
                                       apply_absolute_value=True))
                spread_top(P, 3, top[:, :], fast)
                fast(vec.reciprocal(top_r[:, :], top[:, :]))
                fast(vec.tensor_scalar(top_r[:, :], top_r[:, :], GSCALE, None, ALU.mult))
                vec.sem_inc(S["scaled"], 1)
                for i in range(3):
                    low_part(i + 1, kvs[:, :, i * D:(i + 1) * D], top_r[0:P, i:i + 1], i * D, fast)
                vec.wait_ge(S["rep_ready"], 3)
                fast(vec.tensor_tensor(top_r[:, 0:1], top[:, 0:1], top[:, 1:2], ALU.mult))
                fast(vec.tensor_scalar(top_r[:, 0:1], top_r[:, 0:1], GSCALE ** -2, None, ALU.mult))
                vec.sem_inc(S["parts_ready"], 1)
                edge_layer("l1", fast)
                fast(vec.tensor_scalar(agg[:, 0:T, 0:D], agg[:, 0:T, 0:D], top[0:P, 2:3], 1 / GSCALE, ALU.mult, ALU.mult))
            with vec.Else():
                vec.sem_inc(S["table_ready"], 1)
                gather_aggregate("l1")
            step(vec.tensor_scalar(agg[:, 0:T, D:M1], agg[:, 0:T, D:M1], 1e-8, None, ALU.add))
            step(vec.reciprocal(agg[:, 0:T, D:M1], agg[:, 0:T, D:M1]))
            step(vec.tensor_tensor(h[:, :, :].rearrange("p t (a d) -> p t a d", a=HEADS),
                                   agg[:, 0:T, 0:D].rearrange("p t (a d) -> p t a d", a=HEADS),
                                   agg[:, 0:T, D:M1].unsqueeze(3).to_broadcast([P, T, HEADS, HD]), ALU.mult))
            step(vec.tensor_tensor(xs[:, :, :], xs[:, :, :], h[:, :, :], ALU.add))

            layer_norm()
            with vec.If(way < 1):
                vec.sem_inc(S["scaled"], 1)
                low_part(4, h, GSCALE, 0, fast)
                vec.sem_inc(S["parts_ready"], 1)
                vec.wait_ge(S["wsl_in"], 16)
                fast(vec.tensor_reduce(top_r[:, 0:1], wsl[:, :, 0], AX.X, ALU.max, apply_absolute_value=True))
                spread_top(L, 1, top[:, 0:1], fast)
                fast(vec.reciprocal(top_r[:, 0:1], top[:, 0:1]))
                fast(vec.tensor_scalar(wsl[:, :, 0], wsl[:, :, 0], top_r[:, 0:1], None, ALU.mult))
                edge_layer("l2", fast)
                fast(vec.tensor_scalar(coef[:, :], rdeg[:, :], top[0:P, 0:1], 1 / GSCALE, ALU.mult, ALU.mult))
            with vec.Else():
                vec.sem_inc(S["table_ready"], 1)
                gather_aggregate("l2")
                gen(vec.tensor_copy(coef[:, :], rdeg[:, :]))
            vec.sem_inc(S["l2_done"], 1)
            vec.tensor_tensor(bias2[:, 0:D], bias2[:, 0:D], bias2[:, D:], ALU.add)
            step(vec.tensor_tensor(cat[:, :, D:], agg[:, 0:T, 0:D], per_node(coef), ALU.mult))
            vec.sem_inc(S["h_ready"], 1)
            take(vec, "v", "l2_cat", lambda t, n, b: vec.tensor_copy(
                catT[:, t:t + n, :], ps[:, b, 0:n * P].rearrange("p (t n) -> p t n", t=n)))
            take(vec, "v", "l2_w", lambda t, n, b: vec.tensor_copy(w2[:, :], ps[:, b, 0:D]))
            take(vec, "v", "l2_out", lambda t, n, b: vec.tensor_tensor(
                xs[:, t:t + n, :], xs[:, t:t + n, :], ps[0:P, b, 0:n * D].rearrange("p (t n) -> p t n", t=n), ALU.add))
            all_taken(vec, "l2_out")

            layer_norm(cjs)
            with vec.If(way < 1):
                fast(vec.tensor_reduce(top_r[0:P, 0:1], cjs[:, :], AX.X, ALU.max, apply_absolute_value=True))
                spread_top(P, 1, top[:, 0:1], fast)
                fast(vec.reciprocal(top_r[:, 0:1], top[:, 0:1]))
                fast(vec.tensor_scalar(top_r[:, 0:1], top_r[:, 0:1], GSCALE, None, ALU.mult))
                vec.sem_inc(S["scaled"], 1)
                low_part(5, h, top_r[0:P, 0:1], 0, fast)
                vec.sem_inc(S["parts_ready"], 1)
                edge_layer("l3", fast)
                fast(vec.tensor_scalar(coef[:, :], cis[:, :], top[0:P, 0:1], 1 / GSCALE, ALU.mult, ALU.mult))
            with vec.Else():
                vec.sem_inc(S["table_ready"], 1)
                gather_aggregate("l3")
                gen(vec.tensor_copy(coef[:, :], cis[:, :]))
            step(vec.tensor_tensor(h[:, :, :], agg[:, 0:T, 0:D], per_node(coef), ALU.mult))
            vec.tensor_tensor(xs[:, :, :], xs[:, :, :], h[:, :, :], ALU.add).then_inc(S["out_ready"], 1)

        @block.tensor
        def _(pe):
            passes = [0]

            def gather_aggregate(p):
                w = WIDTH[p]
                b = passes[0] * J
                if passes[0]:
                    pe.wait_ge(S["acc_taken"], passes[0])
                for q in range(NBANK):
                    pe.matmul(acc[0:P, q, :], zeros[:, 0:P], zeros, start=True, stop=True)
                with pe.Fori(0, J) as j:
                    pe.wait_ge(S["msg_ready"], b + 1 + j)
                    pe.wait_ge(S["hit_ready"], b + 1 + j)
                    for t in range(T):
                        last = pe.matmul(acc[0:P, t // TB, (t % TB) * M1:(t % TB) * M1 + w],
                                         hit[:, t * P:(t + 1) * P], msg[:, 0:w], start=False, stop=True,
                                         skip_group_check=True)
                    last.then_inc(S["scattered"], 1)
                passes[0] += 1

            def spread_top(n, k, src_ap, i):
                pe.wait_ge(S["top_go"], i)
                pe.transpose(ps[0:k, 0, 0:n], src_ap, ident[0:n, 0:n]).then_inc(S["top_T"], 1)
                pe.wait_ge(S["top_d"], i)
                pe.matmul(ps[:, 1, 0:k], ones[0:k, :], top_g[0:k, 0:k], start=True, stop=True).then_inc(S["top_all"], 1)

            def edge_layer(p, n_parts):
                groups = GROUPS[p]
                ng = len(groups)
                w = 3 * D if p == "l1" else D
                m1 = 3 * M1 if p == "l1" else 2 * D
                pe.sem_inc(S[p + "_gath"], 2 * ng)
                pe.sem_inc(S[p + "_scat"], 2)
                pe.wait_ge(S["parts_ready"], n_parts)

                def gather(t, par, m, c, n):
                    if m == 0:
                        pe.wait_ge(S[p + "_ohT"], t + (ROOMS[p] + 1))
                    prev = m - RING + 1 + ng if m >= RING else max(k for k in range(ng) if k % RING == m) + 1
                    if p == "l1":
                        pe.wait_ge(S[p + "_rows"], t * ng + prev)
                    elif m == ng - 1:
                        pe.wait_ge(S[p + "_last_rows"], t + 1)
                    else:
                        pe.wait_ge(S[p + "_rows"], t * (ng - 1) + (m + 1))
                    for k in range(c, c + n):
                        o = (k - c) * w
                        a, b = (D, 3 * D) if p == "l1" else (0, D)
                        for i in range(2):
                            rhs = parts[:, k, i, a:b] if k < T else \
                                parts[:, bass.ds(t, 1), i, a:b].rearrange("p t f -> p (t f)")
                            last = pe.matmul(ps[:, m % RING, o:o + b - a], ohT[:, par, 0, k * L:(k + 1) * L], rhs,
                                             start=(i == 0), stop=(i == 1))
                        if p == "l1":
                            for i in range(2):
                                rhs = parts[:, bass.ds(t, 1), i, 0:D].rearrange("p t f -> p (t f)")
                                last = pe.matmul(ps[:, m % RING, o + 2 * D:o + w], ohT[:, par, 1, k * L:(k + 1) * L], rhs,
                                                 start=(i == 0), stop=(i == 1))
                    last.then_inc(S[p + "_gath"], 1)

                def scatter(t, par, c, n):
                    if c == 0:
                        pe.wait_ge(S[p + "_ohd"], t + 1)
                        pe.wait_ge(S[p + "_low"], t + 3)
                        pe.wait_ge(S[p + "_sums"], t + 1)
                    for k in range(c, c + n):
                        last = pe.matmul(ps[0:P, RING + par, 0:m1], ohd[:, par, :, k],
                                         msg1[:, par, k, :] if p == "l1" else msg2[:, par, k, :],
                                         start=(k == 0), stop=(k == C - 1))
                    if c + n == C:
                        last.then_inc(S[p + "_scat"], 1)

                def body(s, par, on):
                    c = 0
                    if 4 in on and p != "l1":
                        scatter(s - 4, par, 0, C)
                    for m, n in enumerate(groups):
                        if 1 in on:
                            gather(s - 1, 1 - par, m, c, n)
                        if 4 in on and p == "l1" and m == RING - 1:
                            scatter(s - 4, par, 0, C)
                        c += n
                tile_steps(pe, body)

            pe.wait_ge(S["pool_step"], 13)
            pe.wait_ge(S["first_d"], 1)
            pe.matmul(ps[0:P, 0, 0:P], ones[0:P, 0:P], first_d, start=True, stop=True).then_inc(S["first_ps"], 1)
            pe.wait_ge(S["link_ready"], 1)
            pe.matmul(ps[0:P, 1, 0:T], link_m, run_end, start=True, stop=True).then_inc(S["carry_ps"], 1)
            pe.wait_ge(S["bad_ready"], 1)
            pe.matmul(ps[0:1, 2, 0:1], run_end[:, 0:1], ones[0:P, 0:1], start=True, stop=True).then_inc(S["bad_ps"], 1)
            way = path(pe)

            with pe.If(way < 1):
                pe.wait_ge(S["place_back"], 16)
                n = BT * JT
                for c in range(3):
                    for b in range(T // BT):
                        last = pe.transpose(ps[0:P, c, b * n:(b + 1) * n],
                                            placed[:, b, :].rearrange("r (p c) -> r c p", c=3)[:, c, :], ident[0:n, 0:n])
                    last.then_inc(S["place_T"], 1)
                pe.sem_inc(S["sorted"], 2)
                pe.matmul(ps[:, 3, 0:TA * C], zero_c[:, 0:L], zero_c[:, 0:TA * C], start=True, stop=True)
                pe.matmul(ps[:, 4, 0:(T - TA + 1) * C], zero_c[:, 0:L], zero_c[:, 0:(T - TA + 1) * C], start=True, stop=True)

                def sort_tile(t, par, early, late):
                    pe.wait_ge(S["to_slot"], t + 2)
                    pe.wait_ge(S["to_lane"], t + 1)
                    for k in range(JT):
                        first, bank = early if k < JH else late
                        o = first * C if bank == 3 else (first - (TA - 1)) * C
                        last = pe.matmul(ps[:, bank, bass.ds(o, W2)], to_lane[:, par, :, k], to_col[:, par, :, k],
                                         start=False, stop=True, skip_group_check=True)
                    last.then_inc(S["sorted"], 1)
                sort_tile(0, 0, (0, 3), (0, 3))
                with pe.Fori(0, (TA - 2) // 2) as i:
                    for u in range(2):
                        sort_tile(i * 2 + (u + 1), (u + 1) % 2, (i * 2 + u, 3), (i * 2 + (u + 1), 3))
                sort_tile(TA - 1, (TA - 1) % 2, (TA - 2, 3), (TA - 1, 4))
                with pe.Fori(0, (T - 1 - TA) // 2) as i:
                    for u in range(2):
                        sort_tile(i * 2 + (TA + u), (TA + u) % 2, (i * 2 + (TA + u - 1), 4), (i * 2 + (TA + u), 4))
                sort_tile(T - 1, (T - 1) % 2, (T - 2, 4), (T - 2, 4))
                pe.wait_ge(S["slots_ready"], 1)
                for e, tab in enumerate((sl, dl_s.rearrange("p s c -> p (s c)"), sl_s.rearrange("p s c -> p (s c)"))):
                    for c in range(QT):
                        k = min(L, Q - c * L)
                        last = pe.transpose(ps[0:k, 2 + 2 * e + c // 4, (c % 4) * L:(c % 4 + 1) * L], tab[:, c * L:c * L + k], ident[:, :])
                        if c in (3, QT - 1):
                            last.then_inc(S["rowT_ps"], 1)
                pe.wait_ge(S["rowT_ready"], 6)
                pe.sem_inc(S["adj_mm"], 7)
                pe.sem_inc(S["adj_done"], 1)
                with pe.Fori(0, T) as d:
                    def degree(k):
                        half, at = (0, k) if k < KG[0] else (1, k - KG[0])
                        return pe.matmul(ps[0:P, 7, 0:1], adj_oh[half][1][:, :, at], ones_b[:, :], start=(k == 0), stop=(k == C - 1))
                    k = 0
                    for g, n in enumerate(AG):
                        if g < 6:
                            pe.wait_ge(S["adj_taken"], d * 6 + (g + 1))
                        for j in range(n):
                            half, at = (0, k) if k < KG[0] else (1, k - KG[0])
                            if at == 0:
                                pe.wait_ge(S["adj_oh"], d * 4 + (2 * half + 2))
                            last = pe.matmul(ps[0:P, g, j * P:(j + 1) * P], adj_oh[half][0][:, :, at], adj_oh[half][1][:, :, at],
                                             start=True, stop=True)
                            if k == KG[0] - 1:
                                pe.wait_ge(S["adj_done"], d + 1)
                                for e in range(KG[0]):
                                    last = degree(e)
                                last.then_inc(S["adj_used"], 1)
                            elif k >= KG[0]:
                                last = degree(k)
                            k += 1
                        last.then_inc(S["adj_mm"], 1)
                pe.sem_inc(S["combined"], 2)

                def combine(n, odd, c):
                    pe.wait_ge(S["mains_taken"], n + (NCH + 1))
                    pe.wait_ge(S["sums_read"], n + 1)
                    for k in range(min(CH, T - CH * c)):
                        last = pe.matmul(ps[0:P, 7, k * D:(k + 1) * D], part[:, odd, k * P:(k + 1) * P], pair[:, :], start=True, stop=True)
                    last.then_inc(S["combined"], 1)

                def iteration(n, u, first):
                    for c in range(NCH):
                        w = min(CH, T - CH * c) * P
                        pe.wait_ge(S["mains_taken"], n + (c + 1))
                        for s in range(T):
                            if c == 0 and s % CH == 0:
                                if s == CH * (NCH // 2) and not first:
                                    combine(n + (-1), (u + 1 + NCH - 1) % 2, NCH - 1)
                                pe.wait_ge(S["hl_ready"], n + (s // CH + 1))
                            last = pe.matmul(ps[:, c, 0:w], hl[0:P, u, s, :], adj[:, s, c * CH * P:c * CH * P + w],
                                             start=(s == 0), stop=(s == T - 1))
                        last.then_inc(S["mains"], 1)
                        if c:
                            combine(n + (c - 1), (u + c - 1) % 2, c - 1)
                iteration(0, 0, True)
                with pe.Fori(0, K0 // 2 - 1) as i:
                    for u in range(2):
                        iteration(i * (2 * NCH) + (u + 1) * NCH, 1 - u, False)
                iteration((K0 - 1) * NCH, 1, False)
                combine(K0 * NCH - 1, (1 + NCH - 1) % 2, NCH - 1)
            with pe.Else():
                pe.wait_ge(S["g_pool"], 2)
                gather_aggregate("deg")
                for _ in range(K0):
                    gather_aggregate("l0")
            pe.wait_ge(S["h_ready"], 1)
            fill("l1_h", lambda t, k, n, b: pe.transpose(ps[0:D, b, k * P:(k + 1) * P], h[:, t, :], ident[0:P, 0:P]))
            all_taken(pe, "l1_h")
            fill("l1_qkv", lambda t, k, n, b: pe.matmul(ps[0:P, b, k * 3 * D:(k + 1) * 3 * D], hT[:, t, :], wqkv[:, :],
                                                       start=True, stop=True))
            with pe.If(way < 1):
                spread_top(P, 3, top_r[0:P, 0:3], 1)
                edge_layer("l1", 1)
                spread_top(L, 1, top_r[:, 0:1], 2)
                edge_layer("l2", 2)
            with pe.Else():
                gather_aggregate("l1")
                gather_aggregate("l2")
            pe.wait_ge(S["h_ready"], 2)
            pe.wait_ge(S["cat_norm"], 1)
            fill("l2_cat", lambda t, k, n, b: pe.transpose(ps[:, b, k * P:(k + 1) * P], cat[:, t, :], ident[0:P, 0:P]))
            fill("l2_w", lambda t, k, n, b: pe.transpose(ps[:, b, 0:D], w2raw[:, :], ident[0:D, 0:D]))
            all_taken(pe, "l2_cat")
            all_taken(pe, "l2_w")

            def outputs(t, k, n, b):
                if k == 0:
                    pe.matmul(ps[0:P, b, 0:n * D].rearrange("p (t n) -> p t n", t=n), ones[0:1, 0:P],
                              bias2[:, 0:D].unsqueeze(1).to_broadcast([1, n, D]), start=True, stop=True)
                return pe.matmul(ps[0:P, b, k * D:(k + 1) * D], catT[:, t, :], w2[:, :],
                                 start=False, stop=True, skip_group_check=True)
            fill("l2_out", outputs)
            with pe.If(way < 1):
                spread_top(P, 1, top_r[0:P, 0:1], 3)
                edge_layer("l3", 3)
            with pe.Else():
                gather_aggregate("l3")


_INS = ['x', 'src', 'dst', 'edge_attr_64', 'edge_weight', 'node_vec1', 'node_vec1_n2', 'L1_gnn_qTrans',
        'L1_gnn_kTrans', 'L1_gnn_vTrans', 'L2_gnn_W_self', 'L2_gnn_b_self', 'L2_gnn_W_neigh',
        'L2_gnn_b_neigh', 'L3_gnn_ps_w']


def kernel(**inputs):
    import numpy as _np
    import concourse.bacc as _bacc
    from concourse import mybir as _mybir
    from concourse.bass_utils import run_bass_kernel_spmd as _run

    nc = _bacc.Bacc("TRN2", target_bir_lowering=False, num_devices=1)
    arrays, args = {}, []
    for name in _INS:
        a = _np.ascontiguousarray(inputs[name])
        arrays[f"in_{name}_dram"] = a
        args.append(nc.dram_tensor(f"in_{name}_dram", a.shape, _mybir.dt.from_np(a.dtype), kind="ExternalInput").ap())
    args.append(nc.dram_tensor("out_dram", (N, D), F32, kind="ExternalOutput").ap())
    graph_net(nc, *args)
    r = _run(nc, [arrays], core_ids=[0])
    return r.results[0]["out_dram"]
```
